# Optimizing a Trainium2 kernel written in Bass

```python
import numpy as np
import jax
import jax.numpy as jnp

def _softmax(x, axis=-1):
    return jax.nn.softmax(x, axis=axis)

def _gelu(x):
    return jax.nn.gelu(x, approximate=True)

def _silu(x):
    return jax.nn.silu(x)

def _sigmoid(x):
    return jax.nn.sigmoid(x)

def _layernorm(x, axis=-1, eps=1e-05):
    m = jnp.mean(x, axis=axis, keepdims=True)
    v = jnp.var(x, axis=axis, keepdims=True)
    return (x - m) / jnp.sqrt(v + eps)

def _scatter_add(tgt, idx, src, axis=0):
    return tgt.at[idx].add(src)

def _segment_sum(src, seg, n):
    return jax.ops.segment_sum(src, seg, n)
kernel_name = 'mk_adaln_ffn_d2_seqx_r8_8e9ffb'

def setup_inputs(seed: int=0):
    np.random.seed(seed)
    _w = jnp.asarray

    def _rec_inputs():
        import jax
        import jax.numpy as jnp
        _rk = jax.random.key(seed)
        x = -0.0002071 + 1 * jax.random.normal(jax.random.fold_in(_rk, 1), (128, 32, 128), jnp.float32)
        _lenS = 32 - jax.random.randint(jax.random.fold_in(_rk, 7), (128,), 0, max(1, 32 // 4) + 1, jnp.int32)
        _lenS2 = 32 - jax.random.randint(jax.random.fold_in(_rk, 8), (128,), 0, max(1, 32 // 4) + 1, jnp.int32)
        cond_8 = jax.random.uniform(jax.random.fold_in(_rk, 11), (128, 8), jnp.float32, 0.0, 0.983423)
        return (x, cond_8)
    x, cond_8 = _rec_inputs()

    def _L0_cond_setup():
        import jax, jax.numpy as jnp
        import numpy as np
        R = 16
        ALPHA = 32.0
        SCALING = ALPHA / R
        key = jax.random.key(seed)
        ks = jax.random.split(key, 6)
        B, T, C, O, E = (16, 1500, 128, 128, 8)
        x = jax.random.normal(ks[0], (B, T, C), dtype=jnp.float32)
        w = jax.random.uniform(ks[1], (B, E), dtype=jnp.float32)
        W_base = jax.random.normal(ks[2], (O, C), dtype=jnp.float32) * 0.02
        b_base = jax.random.normal(ks[3], (O,), dtype=jnp.float32) * 0.02
        As = jax.random.normal(ks[4], (E, R, C), dtype=jnp.float32) * 0.02
        Bs = jax.random.normal(ks[5], (E, O, R), dtype=jnp.float32) * 0.02
        return {'x': x, 'w': w, 'W_base': W_base, 'b_base': b_base, 'As': As, 'Bs': Bs}
    _L0_cond_all = _L0_cond_setup()
    _L0_cond_in = {k: v for k, v in _L0_cond_all.items() if k in ('W_base', 'b_base', 'As', 'Bs')}
    del _L0_cond_all

    def _L0_ffn_setup():
        import jax, jax.numpy as jnp
        import numpy as np
        FEATURES = 128
        D_IN = 128

        def fp8_gemm_optimized(x, input_scale, kernel, kernel_scale):
            s_in = input_scale[0]
            s_k = kernel_scale[0]
            x_q = (x.astype(jnp.float32) / s_in).astype(jnp.float8_e4m3fn)
            k_q = (kernel.astype(jnp.float32) / s_k).astype(jnp.float8_e4m3fn)
            y = jnp.dot(x_q.astype(jnp.float32), k_q.astype(jnp.float32), preferred_element_type=jnp.float32)
            return y * (s_in * s_k)
        key = jax.random.key(seed)
        kx, kk, kb = jax.random.split(key, 3)
        x = jax.random.normal(kx, (4, 1024, D_IN), dtype=jnp.float32)
        limit = np.sqrt(6.0 / (D_IN + FEATURES)).astype(np.float32)
        kernel = jax.random.uniform(kk, (D_IN, FEATURES), dtype=jnp.float32, minval=-limit, maxval=limit).astype(jnp.bfloat16)
        input_scale = jnp.ones((1,), dtype=jnp.float32)
        kernel_scale = jnp.ones((1,), dtype=jnp.float32)
        bias = jnp.zeros((FEATURES,), dtype=jnp.bfloat16)
        return {'x': x, 'kernel': kernel, 'input_scale': input_scale, 'kernel_scale': kernel_scale, 'bias': bias}
    _L0_ffn_all = _L0_ffn_setup()
    _L0_ffn_in = {k: v for k, v in _L0_ffn_all.items() if k in ('kernel', 'input_scale', 'kernel_scale', 'bias')}
    del _L0_ffn_all

    def _L1_cond_setup():
        import jax, jax.numpy as jnp
        import numpy as np
        key = jax.random.key(seed)
        k1, k2, k3, k4, k5 = jax.random.split(key, 5)
        B, N, T, O, G = (32, 32, 128, 128, 8)
        x = jax.random.normal(k1, (B, N, T), dtype=jnp.float32)
        y = jax.random.uniform(k2, (B, G), dtype=jnp.float32)
        weight = jax.random.normal(k3, (G, O, T), dtype=jnp.float32) * (1.0 / np.sqrt(T))
        mask = jax.random.uniform(k4, (O, T), dtype=jnp.float32)
        bias = jax.random.normal(k5, (O,), dtype=jnp.float32)
        return {'x': x, 'y': y, 'weight': weight, 'mask': mask, 'bias': bias}
    _L1_cond_all = _L1_cond_setup()
    _L1_cond_in = {k: v for k, v in _L1_cond_all.items() if k in ('weight', 'mask', 'bias')}
    del _L1_cond_all

    def _L1_ffn_setup():
        import jax, jax.numpy as jnp
        import numpy as np
        B, S, H, NH, E, F = (4, 128, 128, 16, 8, 512)
        D = H // NH
        EPS = 1e-05

        def _layernorm(x, g, b):
            mu = jnp.mean(x, axis=-1, keepdims=True)
            var = jnp.var(x, axis=-1, keepdims=True)
            return (x - mu) * jax.lax.rsqrt(var + EPS) * g + b
        key = jax.random.key(seed)
        ks = jax.random.split(key, 16)
        s = 0.02
        return {'x': jax.random.normal(ks[0], (B, S, H), jnp.float32), 'ln1_g': jnp.ones((H,), jnp.float32), 'ln1_b': jnp.zeros((H,), jnp.float32), 'ln2_g': jnp.ones((H,), jnp.float32), 'ln2_b': jnp.zeros((H,), jnp.float32), 'wq': jax.random.normal(ks[1], (H, H), jnp.float32) * s, 'bq': jnp.zeros((H,), jnp.float32), 'wk': jax.random.normal(ks[2], (H, H), jnp.float32) * s, 'bk': jnp.zeros((H,), jnp.float32), 'wv': jax.random.normal(ks[3], (H, H), jnp.float32) * s, 'bv': jnp.zeros((H,), jnp.float32), 'wo': jax.random.normal(ks[4], (H, H), jnp.float32) * s, 'bo': jnp.zeros((H,), jnp.float32), 'gate_w': jax.random.normal(ks[5], (H, E), jnp.float32) * s, 'gate_b': jnp.zeros((E,), jnp.float32), 'w1': jax.random.normal(ks[6], (E, H, F), jnp.float32) * s, 'b1': jnp.zeros((E, F), jnp.float32), 'w2': jax.random.normal(ks[7], (E, F, H), jnp.float32) * s, 'b2': jnp.zeros((E, H), jnp.float32)}
    _L1_ffn_all = _L1_ffn_setup()
    _L1_ffn_in = {k: v for k, v in _L1_ffn_all.items() if k in ('ln1_g', 'ln1_b', 'ln2_g', 'ln2_b', 'wq', 'bq', 'wk', 'bk', 'wv', 'bv', 'wo', 'bo', 'gate_w', 'gate_b', 'w1', 'b1', 'w2', 'b2')}
    del _L1_ffn_all
    return {'x': x, 'cond_8': cond_8, 'L0_cond_W_base': _L0_cond_in['W_base'], 'L0_cond_b_base': _L0_cond_in['b_base'], 'L0_cond_As': _L0_cond_in['As'], 'L0_cond_Bs': _L0_cond_in['Bs'], 'L0_ffn_kernel': _L0_ffn_in['kernel'], 'L0_ffn_input_scale': _L0_ffn_in['input_scale'], 'L0_ffn_kernel_scale': _L0_ffn_in['kernel_scale'], 'L0_ffn_bias': _L0_ffn_in['bias'], 'L1_cond_weight': _L1_cond_in['weight'], 'L1_cond_mask': _L1_cond_in['mask'], 'L1_cond_bias': _L1_cond_in['bias'], 'L1_ffn_ln1_g': _L1_ffn_in['ln1_g'], 'L1_ffn_ln1_b': _L1_ffn_in['ln1_b'], 'L1_ffn_ln2_g': _L1_ffn_in['ln2_g'], 'L1_ffn_ln2_b': _L1_ffn_in['ln2_b'], 'L1_ffn_wq': _L1_ffn_in['wq'], 'L1_ffn_bq': _L1_ffn_in['bq'], 'L1_ffn_wk': _L1_ffn_in['wk'], 'L1_ffn_bk': _L1_ffn_in['bk'], 'L1_ffn_wv': _L1_ffn_in['wv'], 'L1_ffn_bv': _L1_ffn_in['bv'], 'L1_ffn_wo': _L1_ffn_in['wo'], 'L1_ffn_bo': _L1_ffn_in['bo'], 'L1_ffn_gate_w': _L1_ffn_in['gate_w'], 'L1_ffn_gate_b': _L1_ffn_in['gate_b'], 'L1_ffn_w1': _L1_ffn_in['w1'], 'L1_ffn_b1': _L1_ffn_in['b1'], 'L1_ffn_w2': _L1_ffn_in['w2'], 'L1_ffn_b2': _L1_ffn_in['b2']}

def reference(x, cond_8, L0_cond_W_base, L0_cond_b_base, L0_cond_As, L0_cond_Bs, L0_ffn_kernel, L0_ffn_input_scale, L0_ffn_kernel_scale, L0_ffn_bias, L1_cond_weight, L1_cond_mask, L1_cond_bias, L1_ffn_ln1_g, L1_ffn_ln1_b, L1_ffn_ln2_g, L1_ffn_ln2_b, L1_ffn_wq, L1_ffn_bq, L1_ffn_wk, L1_ffn_bk, L1_ffn_wv, L1_ffn_bv, L1_ffn_wo, L1_ffn_bo, L1_ffn_gate_w, L1_ffn_gate_b, L1_ffn_w1, L1_ffn_b1, L1_ffn_w2, L1_ffn_b2):
    import jax
    import jax.numpy as jnp

    def _L0_cond_ref(x, w, W_base, b_base, As, Bs):
        import jax, jax.numpy as jnp
        import numpy as np
        R = 16
        ALPHA = 32.0
        SCALING = ALPHA / R
        out = jnp.einsum('btc,oc->bto', x, W_base) + b_base
        h = jnp.einsum('btc,erc->bter', x, As)
        lora = jnp.einsum('bter,eor,be->bto', h, Bs, w)
        return out + lora * SCALING

    def _L0_ffn_ref(x, kernel, input_scale, kernel_scale, bias):
        import jax, jax.numpy as jnp
        import numpy as np
        FEATURES = 128
        D_IN = 128

        def fp8_gemm_optimized(x, input_scale, kernel, kernel_scale):
            s_in = input_scale[0]
            s_k = kernel_scale[0]
            x_q = (x.astype(jnp.float32) / s_in).astype(jnp.float8_e4m3fn)
            k_q = (kernel.astype(jnp.float32) / s_k).astype(jnp.float8_e4m3fn)
            y = jnp.dot(x_q.astype(jnp.float32), k_q.astype(jnp.float32), preferred_element_type=jnp.float32)
            return y * (s_in * s_k)
        dtype = jnp.bfloat16
        x = x.astype(dtype)
        orig_shape = x.shape
        x2 = x.reshape(-1, x.shape[-1])
        y = fp8_gemm_optimized(x2, input_scale, kernel, kernel_scale)
        y = y.astype(dtype) + bias
        return y.reshape(orig_shape[:-1] + (FEATURES,))

    def _L1_cond_ref(x, y, weight, mask, bias):
        import jax, jax.numpy as jnp
        import numpy as np
        masked_w = weight * mask[None, :, :]
        w_bot = jnp.einsum('bg,got->bot', y, masked_w)
        return jnp.einsum('bnt,bot->bno', x, w_bot) + bias

    def _L1_ffn_ref(x, ln1_g, ln1_b, ln2_g, ln2_b, wq, bq, wk, bk, wv, bv, wo, bo, gate_w, gate_b, w1, b1, w2, b2):
        import jax, jax.numpy as jnp
        import numpy as np
        B, S, H, NH, E, F = (4, 128, 128, 16, 8, 512)
        D = H // NH
        EPS = 1e-05

        def _layernorm(x, g, b):
            mu = jnp.mean(x, axis=-1, keepdims=True)
            var = jnp.var(x, axis=-1, keepdims=True)
            return (x - mu) * jax.lax.rsqrt(var + EPS) * g + b
        b, s, h = x.shape
        hn = _layernorm(x, ln1_g, ln1_b)
        q = (hn @ wq + bq).reshape(b, s, NH, D).transpose(0, 2, 1, 3)
        k = (hn @ wk + bk).reshape(b, s, NH, D).transpose(0, 2, 1, 3)
        v = (hn @ wv + bv).reshape(b, s, NH, D).transpose(0, 2, 1, 3)
        scores = jnp.einsum('bhqd,bhkd->bhqk', q, k) / jnp.sqrt(jnp.float32(D))
        attn = jax.nn.softmax(scores, axis=-1)
        o = jnp.einsum('bhqk,bhkd->bhqd', attn, v)
        o = o.transpose(0, 2, 1, 3).reshape(b, s, h)
        x = x + (o @ wo + bo)
        hn2 = _layernorm(x, ln2_g, ln2_b).reshape(-1, h)
        logits = hn2 @ gate_w + gate_b
        idx = jnp.argmax(logits, axis=-1)
        mid = jax.nn.relu(jnp.einsum('th,ehf->etf', hn2, w1) + b1[:, None, :])
        y = jnp.einsum('etf,efh->eth', mid, w2) + b2[:, None, :]
        moe = y[idx, jnp.arange(hn2.shape[0])]
        return x + moe.reshape(b, s, h)
    x = x + _L0_ffn_ref(_L0_cond_ref(x, cond_8, L0_cond_W_base, L0_cond_b_base, L0_cond_As, L0_cond_Bs), L0_ffn_kernel, L0_ffn_input_scale, L0_ffn_kernel_scale, L0_ffn_bias)
    x = x + _L1_ffn_ref(_L1_cond_ref(x, cond_8, L1_cond_weight, L1_cond_mask, L1_cond_bias), L1_ffn_ln1_g, L1_ffn_ln1_b, L1_ffn_ln2_g, L1_ffn_ln2_b, L1_ffn_wq, L1_ffn_bq, L1_ffn_wk, L1_ffn_bk, L1_ffn_wv, L1_ffn_bv, L1_ffn_wo, L1_ffn_bo, L1_ffn_gate_w, L1_ffn_gate_b, L1_ffn_w1, L1_ffn_b1, L1_ffn_w2, L1_ffn_b2)
    return x

_drawn_inputs = setup_inputs


def setup_inputs(seed=0):
    import zlib

    import numpy as np

    out = dict(_drawn_inputs(seed))
    spreads = {'L0_ffn_bias': (0.0, 0.1),
     'L1_ffn_ln1_g': (1.0, 0.6),
     'L1_ffn_ln1_b': (0.0, 0.8),
     'L1_ffn_ln2_g': (1.0, 0.2),
     'L1_ffn_ln2_b': (0.0, 0.291),
     'L1_ffn_bq': (0.0, 0.8),
     'L1_ffn_bk': (0.0, 0.8),
     'L1_ffn_bv': (0.0, 0.427),
     'L1_ffn_bo': (0.0, 0.1),
     'L1_ffn_gate_b': (0.0, 0.1),
     'L1_ffn_b1': (0.0, 0.438),
     'L1_ffn_b2': (0.0, 0.1)}
    factors = {'L1_ffn_wq': 8.0, 'L1_ffn_wk': 8.0}
    for name, (base, spread) in spreads.items():
        noise = np.random.default_rng([zlib.crc32(name.encode()), seed]).standard_normal(out[name].shape)
        drawn = base * np.exp(spread * noise) if base else spread * noise
        out[name] = jnp.asarray(drawn.astype(out[name].dtype))
    for name, factor in factors.items():
        out[name] = (out[name] * factor).astype(out[name].dtype)
    return out
```

```python
from contextlib import ExitStack

import numpy as np

import concourse.bass as bass
from concourse import mybir

F32 = mybir.dt.float32
BF16 = mybir.dt.bfloat16
U32 = mybir.dt.uint32
ALU = mybir.AluOpType
ACT = mybir.ActivationFunctionType
AX = mybir.AxisListType

P = 128
B, S, H = 128, 32, 128
N_TOK = B * S
G = 8
R = 16
LORA_SCALE = 2.0
NH, D = 16, 8
E, F = 8, 512
EPS = 1e-5
CHUNK = 512
NC = N_TOK // CHUNK
CB = CHUNK // S
NG = CHUNK // P
GB = P // S
HQ = 4
NI = H // 32
FB = F // P
ROW = 2 * H + 1
REGION = N_TOK + P
NT = N_TOK // P + E
PAD_ID = 65536.0
FP8_MAX_IN = 464.0
F32_MAX = 3.4028234e38
MIX_BANK = (1, 2, 1, 3)
SCHED_STEPS = 23

PACK = [
    [("lora_a", H), ("w_base", H), ("lora_b", H), ("lora_w", B), ("b_base", 1), ("s_in", 1), ("s_k", 1)],
    [("mask_o", 16), ("y_rep", B), ("mix_w", G * H), ("mix_mask", G * H)],
    [("ident", P), ("wq", H), ("wk", H), ("wv", H), ("wo", H), ("gate_w", E), ("ln1_g", 1), ("ln1_b", 1),
     ("ln2_g", 1), ("ln2_b", 1), ("bq", 1), ("bk", 1), ("mask_h", HQ), ("mix_bias", H), ("bv", 1), ("bo", H),
     ("gate_b", E), ("upper", P), ("ids", N_TOK // P), ("region", E), ("rank8", E), ("tile_no", NT),
     ("expert_no", E)],
    [("w1", E * (F + FB)), ("w2", E * F), ("b2", E * H)],
]
WIDTH = [sum(w for _, w in part) for part in PACK]


def build(nc, x_t, packs, kernel8, bias8, out):
    ctx = ExitStack()
    with ctx:
        def sb(name, shape, dt=F32):
            return ctx.enter_context(nc.sbuf_tensor(name, shape, dt))

        names = """in0 in1 in2 in3 in8 consts mix_masked setup setup2 bias_mm x_in0 x_in1
            h_mm hs u_mm u_out uv uvs pow2 guard gv q8 y_mm y_out yb2 x1 ybd wb_mm wb_out
            z_mm x1_tr x1_tok z ln1 rstd1 nmr1 hn hn_tr hn_t qkv_mm q_out kx_out v_out zb
            s_mm smax ssub sexp st sums rsum recip rcx pv_mm rt_mm diag0 diag o_t
            wo_mm xp ln2 rstd2 nmr2 hn2 resid tr2 hn2_t gate_mm pick rank_mm ids slot scattered
            sched pads rows_in0 rows_in1 rows_in2 rows_in3 w1_staged t_tr t_xt mid_mm relu_a relu_v out_mm
            fin_pre fin stored0 stored1 held_pe held_dve held_pool""".split()
        sem = {n: ctx.enter_context(nc.semaphore(n)) for n in names}

        def wait(eng, name, value):
            if isinstance(value, int) and value <= 0:
                return
            eng.wait_ge(sem[name], value)

        def wait_turn(eng, name, s, u, turns):
            wait(eng, f"{name}{u}", (16 // turns) * (s - u) + 16)

        def hold(eng, name):
            eng.sem_inc(sem[name], 1)

        pk = [sb(f"pack{n}_sb", [P, w]) for n, w in enumerate(WIDTH)]
        col = {}
        for n, part in enumerate(PACK):
            at = 0
            for name, w in part:
                col[name] = pk[n][:, at:at + w]
                at += w
        k8_in = sb("k8_in", [P, H], BF16)
        bias8_in = sb("bias8_in", [P, 1], BF16)
        k8 = sb("k8", [P, H], BF16)
        bias8f = sb("bias8f", [P, 1])
        r_in = sb("r_in", [P, 1])
        r_k = sb("r_k", [P, 1])
        s_out = sb("s_out", [P, 1])
        bk_mask = sb("bk_mask", [P, HQ])
        minus_half = sb("minus_half", [P, NG])
        ones_b = sb("ones_b", [P, P], BF16)
        upper_b = sb("upper_b", [P, P], BF16)
        pad = sb("pad", [P, ROW])
        base = sb("base", [P, 2, E])

        xb = sb("xb", [P, 2, CHUNK])
        hs = sb("hs", [P, CHUNK])
        ub = sb("ub", [P, CHUNK], BF16)
        uv = sb("uv", [P, CHUNK])
        uvs = sb("uvs", [P, CHUNK])
        magic = sb("magic", [P, CHUNK])
        guard = sb("guard", [P, CHUNK])
        gv = sb("gv", [P, CHUNK])
        x1_tok = sb("x1_tok", [P, 2, CHUNK])
        nmr = sb("nmr", [P, NG])
        nmr2 = sb("nmr2", [P, NG])
        r_in20 = sb("r_in20", [P, 1])
        bv_b = sb("bv_b", [P, H])
        bo2 = sb("bo2", [P, H])
        r64 = sb("r64", [P, NG * NH])
        q8 = sb("q8", [P, CHUNK], BF16)
        yb = sb("yb", [P, CHUNK], BF16)
        yb2 = sb("yb2", [P, CHUNK], BF16)
        x1 = sb("x1", [P, 2, CHUNK])
        ybd = sb("ybd", [P, 16, CB])
        wb = sb("wb", [P, CB, H])
        z = sb("z", [P, CHUNK])
        zb = sb("zb", [P, 2, CHUNK])
        bn = sb("bn", [P, NG, 6])
        mv = sb("mv", [P, NG, 2])
        rs = sb("rs", [P, 2, NG])
        hn = sb("hn", [P, CHUNK])
        hn_t = sb("hn_t", [P, CHUNK])
        qt = sb("qt", [P, CHUNK])
        kx = sb("kx", [P, CB, HQ, S])
        v = sb("v", [P, NG, H])
        mx = sb("mx", [P, NI * NG * HQ])
        pr = sb("pr", [P, NI, NG * HQ * S])
        pt = sb("pt", [P, NI, NG * HQ * S])
        t16 = sb("t16", [P, 64, 16])
        t8 = sb("t8", [P, 64, 8])
        t4 = sb("t4", [P, 64, 4])
        t1 = sb("t1", [P, 64])
        rc = sb("rc", [P, NG * NH, D])
        acc = sb("acc", [P, GB * NG, S])
        o_t = sb("o_t", [P, NG, GB, S])
        xp = sb("xp", [P, CHUNK])
        bn2 = sb("bn2", [P, NG, 6])
        mv2 = sb("mv2", [P, NG, 2])
        rs2 = sb("rs2", [P, 2, NG])
        rows = sb("rows", [P, NG, ROW])
        hn2_t = sb("hn2_t", [P, CHUNK])
        lg = sb("lg", [P, NG, E])
        lmax = sb("lmax", [P, NG])
        oh = sb("oh", [P, NG, E])
        oh_b = sb("oh_b", [P, NG, E], BF16)
        pos = sb("pos", [P, NG, E])
        slot_f = sb("slot_f", [P, NG])
        slot = sb("slot", [P, NG], U32)

        sched = {n: sb(f"sched_{n}", shape) for n, shape in dict(
            n=[1, E], t=[1, E], c0=[1, 2 * E], c1=[1, 2 * E], c2=[1, 2 * E], c3=[1, 2 * E], off=[1, E],
            ge=[1, NT, E], lt=[1, NT, E], at=[1, NT, E], row=[1, NT], expert=[1, NT], none=[1, NT]).items()}
        tiles_u = sb("tiles_u", [1, E], U32)
        pad_row = sb("pad_row", [1, E], U32)
        tile_row = sb("tile_row", [1, NT], U32)
        tile_expert = sb("tile_expert", [1, NT], U32)
        rin = [sb(f"rin{n}", [P, ROW]) for n in range(4)]
        xt = [sb(f"xt{n}", [P, P]) for n in range(2)]
        w1s = [sb(f"w1s{n}", [P, F + FB]) for n in range(2)]
        mid = [sb(f"mid{n}", [P, FB, P]) for n in range(2)]
        res = [sb(f"res{n}", [P, H]) for n in range(2)]
        ob = [sb(f"ob{n}", [P, H]) for n in range(2)]
        id_u = [sb(f"id_u{n}", [P, 1], U32) for n in range(2)]

        so = ctx.enter_context(nc.psum_tensor("so", [P, 4, 512], F32))
        dn = [ctx.enter_context(nc.psum_tensor(f"d{n}", [P, 512], F32)) for n in range(4)]

        routed = nc.dram_tensor("routed", [(E + 1) * REGION, ROW], F32).ap()

        def groups(ap):
            return ap.rearrange("p (g n) -> p g n", g=NG)

        def over_groups(ap):
            return ap.unsqueeze(1).to_broadcast([P, NG, ap.shape[1]])

        def heads_out(h):
            return so[:, :, :].rearrange("p b (g h s) -> p (b g) h s", g=NG, h=HQ)[:, :, h, :]

        def setup_dve(dve):
            done = sem["setup"]
            dve.memset(ones_b[:, :], 1.0).then_inc(done, 1)
            dve.wait_ge(sem["in0"], 16)
            dve.wait_ge(sem["in8"], 32)
            dve.reciprocal(r_in[:, :], col["s_in"]).then_inc(done, 1)
            dve.reciprocal(r_k[:, :], col["s_k"]).then_inc(done, 1)
            dve.scalar_tensor_tensor(s_out[:, :], col["s_in"], -(2.0 ** 20), col["s_k"], ALU.mult,
                                     ALU.mult).then_inc(done, 1)
            dve.tensor_copy(bias8f[:, :], bias8_in[:, :]).then_inc(done, 1)
            dve.tensor_scalar(col["lora_w"], col["lora_w"], LORA_SCALE, None, ALU.mult).then_inc(done, 1)
            dve.wait_ge(done, 6)
            dve.tensor_scalar(r_in20[:, :], r_in[:, :], 2.0 ** -20, None, ALU.mult).then_inc(done, 1)
            dve.tensor_scalar(uv[:, 0:H], k8_in[:, :], r_k[:, 0:1], None, ALU.mult).then_inc(done, 1)
            dve.wait_ge(done, 8)
            dve.tensor_scalar(magic[:, 0:H].bitcast(U32), uv[:, 0:H].bitcast(U32), 0x7F800000, None,
                              ALU.bitwise_and).then_inc(done, 1)
            dve.tensor_scalar(guard[:, 0:H], uv[:, 0:H], F32_MAX / FP8_MAX_IN, 0.0, ALU.mult,
                              ALU.mult).then_inc(done, 1)
            dve.wait_ge(done, 10)
            dve.tensor_scalar(magic[:, 0:H], magic[:, 0:H], 2.0 ** -6, 1.5 * 2.0 ** 20, ALU.max,
                              ALU.mult).then_inc(done, 1)
            dve.wait_ge(done, 11)
            dve.tensor_tensor(magic[:, 0:H], magic[:, 0:H], guard[:, 0:H], ALU.add).then_inc(done, 1)
            dve.wait_ge(done, 12)
            dve.tensor_tensor(uv[:, 0:H], uv[:, 0:H], magic[:, 0:H], ALU.add).then_inc(done, 1)
            dve.wait_ge(done, 13)
            dve.tensor_tensor(k8[:, :], uv[:, 0:H], magic[:, 0:H], ALU.subtract).then_inc(done, 1)
            dve.wait_ge(done, 14)

        def setup2_dve(dve):
            done = sem["setup2"]
            dve.wait_ge(sem["in2"], 16)
            dve.tensor_scalar(bv_b[:, :], ones_b[:, :], col["bv"], None, ALU.mult).then_inc(done, 1)
            dve.tensor_scalar(bk_mask[:, :], col["mask_h"], col["bk"], None, ALU.mult).then_inc(done, 1)
            dve.tensor_copy(upper_b[:, :], col["upper"]).then_inc(done, 1)
            dve.tensor_copy(base[:, 0, :], col["region"]).then_inc(done, 1)
            dve.wait_ge(sem["bias_mm"], 1)
            dve.tensor_tensor(bo2[:, :], dn[3][:, 0:H], col["bo"], ALU.add).then_inc(done, 1)

        LOOP = range(4, NT - 4, 4)

        def tiles(eng, step):
            for s in range(4):
                step(s, s)
            with eng.Fori(0, len(LOOP)) as i:
                for u in range(4):
                    step(4 * i + (4 + u), u)
            for s in range(NT - 4, NT):
                step(s, s % 4)

        def last(s, ahead):
            return isinstance(s, int) and s + ahead >= NT

        def moe_sp(sp):
            sp.wait_ge(sem["sched"], 1)
            for e in range(E):
                row = sp.value_load(pad_row[0:1, e:e + 1], min_val=0, max_val=E * REGION)
                sp.dma_start(routed[bass.ds(row, P), :], pad[:, :]).then_inc(sem["pads"], 16)
            sp.wait_ge(sem["pads"], 16 * (E + 1))
            sp.wait_ge(sem["scattered"], 16 * NG * NC)
            sp.wait_ge(sem["sched"], SCHED_STEPS)

            def step(s, u):
                row = sp.value_load(tile_row[0:1, bass.ds(s, 1)], min_val=0, max_val=E * REGION)
                wait(sp, "fin", s - 3)
                sp.dma_start(rin[u][:, :], routed[bass.ds(row, P), :]).then_inc(sem[f"rows_in{u}"], 16)

            tiles(sp, step)

        def moe_pe(pe):
            def turn(s, u):
                wait_turn(pe, "rows_in", s, u, 4)
                wait(pe, "t_xt", s - 1)
                pe.transpose(dn[u % 2][:, 0:P], rin[u][:, 0:H], col["ident"]).then_inc(sem["t_tr"], 1)

            def hidden(s, u):
                wait(pe, "t_xt", s + 1)
                wait(pe, "w1_staged", s + 1)
                wait(pe, "relu_a", 2 * (s - 1))
                wait(pe, "relu_v", 2 * (s - 1))
                for k in range(FB):
                    mm = pe.matmul(so[:, 2 * (k // 2) + u % 2, (k % 2) * P:(k % 2 + 1) * P],
                                   w1s[u % 2][:, k * P:(k + 1) * P], xt[u % 2][:, :], start=True, stop=True)
                mm.then_inc(sem["mid_mm"], 1)

            def output(s, u):
                e = pe.value_load(tile_expert[0:1, bass.ds(s, 1)], min_val=0, max_val=E - 1)
                wait(pe, "relu_a", 2 * (s + 1))
                wait(pe, "relu_v", 2 * (s + 1))
                wait(pe, "fin", s - 1)
                for k in range(FB):
                    mm = pe.matmul(dn[2 + u % 2][:, 0:H], mid[u % 2][:, k, :],
                                   col["w2"][:, bass.ds(e * F + k * H, H)], start=(k == 0), stop=(k == FB - 1))
                mm.then_inc(sem["out_mm"], 1)

            def step(s, u):
                if not last(s, 1):
                    hidden(s + 1, (u + 1) % 4)
                output(s, u)
                if not last(s, 2):
                    turn(s + 2, (u + 2) % 4)

            pe.wait_ge(sem["slot"], 5 * NC)
            pe.wait_ge(sem["resid"], NC)
            pe.wait_ge(sem["o_t"], NC)
            pe.wait_ge(sem["hn2_t"], NC)
            pe.wait_ge(sem["sched"], SCHED_STEPS)
            turn(0, 0)
            hidden(0, 0)
            turn(1, 1)
            tiles(pe, step)

        def moe_act(act):
            def normed(s, u):
                wait(act, "t_tr", s + 1)
                wait(act, "mid_mm", s - 1)
                act.activation(xt[u % 2][:, :], dn[u % 2][:, 0:P], ACT.Identity, bias=col["ln2_b"],
                               scale=col["ln2_g"]).then_inc(sem["t_xt"], 1)

            def relu(s, u):
                wait(act, "mid_mm", s + 1)
                wait(act, "out_mm", s - 1)
                for k in range(2):
                    act.activation(mid[u % 2][:, k, :], so[:, u % 2, k * P:(k + 1) * P], ACT.Relu,
                                   bias=w1s[u % 2][:, F + k:F + k + 1]).then_inc(sem["relu_a"], 1)

            def step(s, u):
                if not last(s, 1):
                    relu(s + 1, (u + 1) % 4)
                if not last(s, 2):
                    normed(s + 2, (u + 2) % 4)

            normed(0, 0)
            relu(0, 0)
            normed(1, 1)
            tiles(act, step)

        def moe_dve(dve):
            count = [0]

            def link(ins):
                count[0] += 1
                ins.then_inc(sem["sched"], 1)
                dve.wait_ge(sem["sched"], count[0])

            def wide(ap):
                return ap.unsqueeze(2).to_broadcast([1, NT, E])

            def long(ap):
                return ap.unsqueeze(1).to_broadcast([1, NT, E])

            t = sched
            dve.wait_ge(sem["slot"], 5 * NC)
            link(dve.tensor_copy(pad_row[:, :], base[0:1, 0, :]))
            link(dve.tensor_tensor(t["n"][:, :], base[0:1, 0, :], col["region"][0:1, :], ALU.subtract))
            link(dve.tensor_scalar(tiles_u[:, :], t["n"][:, :], 1.0 / P, (P - 1) / P - 0.5 + 0.5 / P, ALU.mult, ALU.add))
            for n in range(4):
                link(dve.memset(t[f"c{n}"][:, :], 0.0))
            link(dve.tensor_copy(t["c0"][:, E:2 * E], tiles_u[:, :]))
            for n in range(3):
                a, b = t[f"c{n}"], t[f"c{n + 1}"]
                link(dve.tensor_tensor(b[:, E:2 * E], a[:, E:2 * E], a[:, E - 2 ** n:2 * E - 2 ** n], ALU.add))
            before, after = t["c3"][:, E - 1:2 * E - 1], t["c3"][:, E:2 * E]
            link(dve.scalar_tensor_tensor(t["off"][:, :], before, -float(P), col["region"][0:1, :], ALU.mult, ALU.add))
            tile_no = col["tile_no"][0:1, :]
            link(dve.tensor_tensor(t["ge"][:, :, :], wide(tile_no), long(before), ALU.is_ge))
            link(dve.tensor_tensor(t["lt"][:, :, :], wide(tile_no), long(after), ALU.is_lt))
            link(dve.tensor_tensor(t["ge"][:, :, :], t["ge"][:, :, :], t["lt"][:, :, :], ALU.mult))
            link(dve.scalar_tensor_tensor(t["at"][:, :, :], wide(tile_no), float(P), long(t["off"][:, :]), ALU.mult, ALU.add))
            link(dve.tensor_tensor(t["at"][:, :, :], t["at"][:, :, :], t["ge"][:, :, :], ALU.mult))
            link(dve.tensor_reduce(t["row"][:, :], t["at"][:, :, :], AX.X, ALU.add))
            link(dve.tensor_tensor(t["lt"][:, :, :], t["ge"][:, :, :], long(col["expert_no"][0:1, :]), ALU.mult))
            link(dve.tensor_reduce(t["expert"][:, :], t["lt"][:, :, :], AX.X, ALU.add))
            link(dve.tensor_scalar(t["none"][:, :], tile_no, t["c3"][:, 2 * E - 1:2 * E], float(E * REGION),
                                   ALU.is_ge, ALU.mult))
            link(dve.tensor_copy(tile_expert[:, :], t["expert"][:, :]))
            link(dve.tensor_tensor(tile_row[:, :], t["row"][:, :], t["none"][:, :], ALU.add))

            def relu(s, u):
                wait(dve, "mid_mm", s + 1)
                wait(dve, "out_mm", s - 1)
                for k in range(2, 4):
                    dve.tensor_scalar(mid[u % 2][:, k, :], so[:, 2 + u % 2, (k - 2) * P:(k - 1) * P],
                                      w1s[u % 2][:, F + k:F + k + 1], 0.0, ALU.add, ALU.max).then_inc(sem["relu_v"], 1)

            def finish(s, u):
                e = dve.value_load(tile_expert[0:1, bass.ds(s, 1)], min_val=0, max_val=E - 1)
                wait_turn(dve, "rows_in", s, u, 4)
                dve.tensor_tensor(res[u % 2][:, :], rin[u][:, H:2 * H], col["b2"][:, bass.ds(e * H, H)],
                                  ALU.add).then_inc(sem["fin_pre"], 1)
                wait(dve, f"stored{u % 2}", 8 * (s - u % 2))
                dve.tensor_copy(id_u[u % 2][:, :], rin[u][:, 2 * H:ROW]).then_inc(sem["fin_pre"], 1)
                wait(dve, "fin_pre", 2 * (s + 1))
                wait(dve, "out_mm", s + 1)
                dve.tensor_tensor(ob[u % 2][:, :], dn[2 + u % 2][:, 0:H], res[u % 2][:, :],
                                  ALU.add).then_inc(sem["fin"], 1)

            def stage(s, u):
                e = dve.value_load(tile_expert[0:1, bass.ds(s, 1)], min_val=0, max_val=E - 1)
                wait(dve, "mid_mm", s - 1)
                wait(dve, "relu_a", 2 * (s - 1))
                wait(dve, "relu_v", 2 * (s - 1))
                dve.tensor_copy(w1s[u % 2][:, :], col["w1"][:, bass.ds(e * (F + FB), F + FB)]).then_inc(sem["w1_staged"], 1)

            def step(s, u):
                if not last(s, 1):
                    relu(s + 1, (u + 1) % 4)
                if not last(s, 2):
                    stage(s + 2, (u + 2) % 4)
                finish(s, u)

            dve.wait_ge(sem["in3"], 16)
            stage(0, 0)
            stage(1, 1)
            relu(0, 0)
            tiles(dve, step)

        def moe_pool(pool):
            def step(s, u):
                wait(pool, "fin", s + 1)
                hold(pool, "held_pool")
                pool.indirect_dma_start(out, bass.IndirectOffsetOnAxis(id_u[u % 2][:, 0:1], 0), ob[u % 2][:, :], None,
                                        bounds_check=N_TOK - 1, oob_is_err=False).then_inc(sem[f"stored{u % 2}"], 16)

            tiles(pool, step)
            for u in range(2):
                pool.wait_ge(sem[f"stored{u}"], 16 * NT // 2)

        block = ctx.enter_context(nc.Block())

        def run(eng, iteration, between=None):
            iteration(0, None, None, None, 0)
            if between:
                between(eng)
            iteration(1, 0, None, None, 1)
            iteration(2, 1, 0, None, 0)
            loops = (NC - 3) // 2
            with eng.Fori(0, loops) as i:
                for u in range(2):
                    m = 2 * i + u
                    iteration(m + 3, m + 2, m + 1, m, (u + 1) % 2)
            for m in range(2 * loops, NC):
                iteration(*(c if c < NC else None for c in (m + 3, m + 2, m + 1)), m, (m + 1) % 2)

        @block.sync
        def _(sp):
            sp.dma_start(pk[0][:, :], packs[0]).then_inc(sem["in0"], 16)
            sp.dma_start(k8_in[:, :], kernel8).then_inc(sem["in8"], 16)
            sp.dma_start(bias8_in[:, :], bias8).then_inc(sem["in8"], 16)

            def iteration(a, n, j, m, p):
                if a is not None:
                    wait(sp, "x1", a - 1)
                    sp.dma_start(xb[:, p, :], x_t[:, bass.ds(a * CHUNK, CHUNK)]).then_inc(sem[f"x_in{p}"], 16)
                if isinstance(a, int) and a < 3:
                    sp.dma_start(pk[a + 1][:, :], packs[a + 1]).then_inc(sem[f"in{a + 1}"], 16)

            run(sp, iteration)
            sp.wait_ge(sem["consts"], 4)
            sp.dma_start(routed[E * REGION:E * REGION + P, :], pad[:, :]).then_inc(sem["pads"], 16)
            moe_sp(sp)

        @block.tensor
        def _(pe):
            def mix(a, k):
                for u in range(2):
                    blk = 2 * k + u
                    mm = pe.matmul(dn[MIX_BANK[k]][:, u * 256:(u + 1) * 256], col["mix_w"][:, blk * P:(blk + 1) * P],
                                   ybd[:, :, :].rearrange("p o b -> p (o b)"), start=True, stop=True)
                mm.then_inc(sem["wb_mm"], 1)

            def values(j, blocks):
                for i in blocks:
                    wait(pe, "st", NI * j + i + 1)
                    hold(pe, "held_pe")
                    for g in range(NG):
                        for b in range(GB):
                            f = slice(32 * b, 32 * b + 32)
                            mm = pe.matmul(so[32 * i:32 * i + 32, b, g * P:(g + 1) * P],
                                           v[f, g, 32 * i:32 * i + 32], pt[f, i, g * P:(g + 1) * P],
                                           start=True, stop=True, tile_position=(32 * b, 32 * i))
                return mm

            def iteration(a, n, j, m, p):
                q = 1 - p
                if a is not None:
                    wait_turn(pe, "x_in", a, p, 2)
                    wait(pe, "q_out", a - 1)
                    pe.matmul(dn[0][:, :], col["lora_a"], xb[:, p, :], start=True, stop=True).then_inc(sem["h_mm"], 1)
                if m is not None:
                    wait(pe, "o_t", m + 1)
                    wait(pe, "v_out", m + 2 if not isinstance(m, int) else min(m + 2, NC))
                    wait(pe, "hn2_t", m)
                    for g in range(NG):
                        mm = pe.matmul(dn[3][:, g * P:(g + 1) * P], o_t[:, g, :, :].rearrange("p b s -> p (b s)"),
                                       col["wo"], start=True, stop=True)
                    mm.then_inc(sem["wo_mm"], 1)
                if a is not None:
                    wait(pe, "y_out", a)
                    pe.matmul(dn[2][:, :], col["w_base"], xb[:, p, :], start=True, stop=False)
                    wait(pe, "hs", a + 1)
                    pe.matmul(dn[2][:, :], col["lora_b"], hs[:, :], start=False, stop=True).then_inc(sem["u_mm"], 1)
                if j is not None:
                    wait(pe, "o_t", j)
                    wait(pe, "q_out", j + 1)
                    wait(pe, "kx_out", HQ * (j + 1))
                    hold(pe, "held_pe")
                    for i in range(NI):
                        f = slice(32 * i, 32 * i + 32)
                        for g in range(NG):
                            for b in range(GB):
                                mm = pe.matmul(so[32 * b:32 * b + 32, i, g * P:(g + 1) * P],
                                               qt[f, (g * GB + b) * S:(g * GB + b + 1) * S],
                                               kx[f, g * GB + b, :, :].rearrange("p h s -> p (h s)"),
                                               start=True, stop=True, tile_position=(32 * i, 32 * b))
                        mm.then_inc(sem["s_mm"], 1)
                if n is not None:
                    wait(pe, "x1", n + 1)
                    wait(pe, "wb_out", 4 * (n + 1))
                    wait(pe, "hs", a + 1 if a is not None else NC)
                    wait(pe, "q_out", n)
                    for g in range(NG):
                        for b in range(GB):
                            c = g * GB + b
                            mm = pe.matmul(dn[0][32 * b:32 * b + 32, g * P:(g + 1) * P],
                                           x1[:, q, c * S:(c + 1) * S], wb[:, c, :], start=True, stop=True)
                    mm.then_inc(sem["z_mm"], 1)
                if m is not None:
                    wait(pe, "hn2", NG * (m + 1))
                    wait(pe, "xp", m + 1)
                    for g in range(NG):
                        mm = pe.transpose(dn[3][:, g * P:(g + 1) * P], rows[:, g, 0:H], col["ident"])
                    mm.then_inc(sem["tr2"], 1)
                if a is not None:
                    wait(pe, "ybd", a + 1)
                    wait(pe, "kx_out", HQ * (a - 1))
                    pe.wait_ge(sem["mix_masked"], 1)
                    mix(a, 0)
                    wait(pe, "u_out", a + 1)
                    mix(a, 1)
                if m is not None:
                    wait(pe, "hn2_t", m + 1)
                    if n is not None:
                        wait(pe, "z", n + 1)
                    else:
                        wait(pe, "q_out", NC)
                        wait(pe, "slot", 5 * m)
                    for g in range(NG):
                        mm = pe.matmul(dn[0][:, g * E:(g + 1) * E], hn2_t[:, g * P:(g + 1) * P], col["gate_w"],
                                       start=True, stop=True)
                    mm.then_inc(sem["gate_mm"], 1)
                if j is not None:
                    values(j, range(0, 2))
                if a is not None:
                    wait(pe, "wb_out", 4 * a + 1)
                    mix(a, 2)
                if n is not None:
                    wait(pe, "v_out", n)
                    if m is not None:
                        wait(pe, "hn2_t", m + 1)
                    for g in range(NG):
                        mm = pe.transpose(dn[3][:, g * P:(g + 1) * P], x1[:, q, g * P:(g + 1) * P], col["ident"])
                    mm.then_inc(sem["x1_tr"], 1)
                if j is not None:
                    values(j, range(2, 3))
                if n is not None:
                    wait(pe, "hn", NG * (n + 1))
                    wait(pe, "wb_out", 4 * a + 2 if a is not None else 4 * NC)
                    wait(pe, "y_out", a if a is not None else NC)
                    for g in range(NG):
                        mm = pe.transpose(dn[2][:, g * P:(g + 1) * P], hn[:, g * P:(g + 1) * P], col["ident"])
                    mm.then_inc(sem["hn_tr"], 1)
                if j is not None:
                    values(j, range(3, NI)).then_inc(sem["pv_mm"], 1)
                if m is not None:
                    wait(pe, "pick", 6 * (m + 1))
                    pe.matmul(dn[0][:, 64:64 + NG * E], upper_b[:, :], oh_b[:, :, :].rearrange("p g e -> p (g e)"),
                              start=True, stop=False, skip_group_check=True)
                    for g in range(NG):
                        mm = pe.matmul(dn[0][:, 64 + (g + 1) * E:64 + (NG + 1) * E].rearrange("p (g e) -> p g e", e=E),
                                       ones_b[:, :], oh_b[:, g, :].unsqueeze(1).to_broadcast([P, NG - g, E]),
                                       start=False, stop=(g == NG - 1), skip_group_check=True)
                    mm.then_inc(sem["rank_mm"], 1)
                if a is not None:
                    if n is not None:
                        wait(pe, "x1_tok", n + 1)
                    mix(a, 3)
                if n is not None:
                    wait(pe, "hn_t", n + 1)
                    if m is not None:
                        wait(pe, "slot", 5 * m + 2)
                    pe.matmul(dn[0][:, :], col["wq"], hn_t[:, :], start=True, stop=True).then_inc(sem["qkv_mm"], 1)
                if j is not None:
                    wait(pe, "rcx", j + 1)
                    wait(pe, "hn_t", n + 1 if n is not None else NC)
                    for g in range(NG):
                        mm = pe.transpose(dn[2][:, g * P:(g + 1) * P],
                                          rc[:, g * NH:(g + 1) * NH, :].rearrange("p h d -> p (h d)"), col["ident"])
                    mm.then_inc(sem["rt_mm"], 1)
                if n is not None:
                    wait(pe, "wb_out", 4 * a + 4 if a is not None else 4 * NC)
                    wait(pe, "x1_tok", n + 1)
                    for g in range(NG):
                        mm = pe.matmul(dn[3][:, g * P:(g + 1) * P], hn_t[:, g * P:(g + 1) * P], col["wv"],
                                       start=True, stop=True)
                    mm.then_inc(sem["qkv_mm"], 1)
                    wait(pe, "kx_out", HQ * n)
                    pe.matmul(dn[1][:, :], col["wk"], hn_t[:, :], start=True, stop=True).then_inc(sem["qkv_mm"], 1)
                if a is not None:
                    wait(pe, "q8", 2 * (a + 1))
                    wait(pe, "wb_out", 4 * a + 2)
                    if n is not None:
                        wait(pe, "hn_t", n + 1)
                    if j is not None:
                        wait(pe, "o_t", j + 1)
                    pe.matmul(dn[2][:, :], k8[:, :], q8[:, :], start=True, stop=True).then_inc(sem["y_mm"], 1)

            def between(pe):
                pe.wait_ge(sem["setup2"], 1)
                pe.wait_ge(sem["wb_out"], 4)
                pe.matmul(dn[3][:, 0:H], bv_b[:, :], col["wo"], start=True, stop=True).then_inc(sem["bias_mm"], 1)
                pe.wait_ge(sem["setup2"], 5)

            pe.wait_ge(sem["setup"], 14)
            run(pe, iteration, between)
            moe_pe(pe)

        @block.scalar
        def _(act):
            def exponentials(j, blocks):
                for i in blocks:
                    wait(act, "ssub", NI * j + i + 1)
                    act.activation(pr[:, i, :], pr[:, i, :], ACT.Exp, scale=float(D) ** -0.5).then_inc(sem["sexp"], 1)

            def mix_out(a, k):
                wait(act, "wb_mm", 4 * a + k + 1)
                wait(act, "z_mm", a)
                act.activation(wb[:, :, 32 * k:32 * k + 32].rearrange("p b (u o) -> p b u o", u=2),
                               dn[MIX_BANK[k]][:, :].rearrange("p (u o b) -> p b u o", u=2, o=16),
                               ACT.Copy).then_inc(sem["wb_out"], 1)

            def iteration(a, n, j, m, p):
                q = 1 - p
                if a is not None:
                    wait(act, "u_mm", a + 1)
                    act.activation(ub[:, :], dn[2][:, :], ACT.Identity, bias=col["b_base"]).then_inc(sem["u_out"], 1)
                    wait(act, "u_out", a + 1)
                    wait(act, "pow2", a)
                    wait(act, "guard", a)
                    act.activation(uv[:, :], ub[:, :], ACT.Copy, scale=r_in[:, 0:1]).then_inc(sem["uv"], 1)
                    wait(act, "gv", a)
                    act.activation(uvs[:, :], ub[:, :], ACT.Copy, scale=r_in20[:, 0:1]).then_inc(sem["uvs"], 1)
                if j is not None:
                    exponentials(j, range(0, 1))
                if m is not None:
                    wait(act, "nmr2", m + 1)
                    wait(act, "scattered", 16 * NG * m)
                    for g in range(NG):
                        act.activation(rows[:, g, 0:H], xp[:, g * P:(g + 1) * P], ACT.Identity,
                                       bias=nmr2[:, g:g + 1], scale=rs2[:, 1, g:g + 1]).then_inc(sem["hn2"], 1)
                if j is not None:
                    exponentials(j, range(1, NI))
                if m is not None:
                    wait(act, "tr2", m + 1)
                    wait(act, "gate_mm", m)
                    act.activation(hn2_t[:, :], dn[3][:, :], ACT.Identity, bias=col["ln2_b"],
                                   scale=col["ln2_g"]).then_inc(sem["hn2_t"], 1)
                if a is not None:
                    mix_out(a, 0)
                    mix_out(a, 1)
                if n is not None:
                    wait(act, "nmr1", n + 1)
                    wait(act, "hn_tr", n)
                    for g in range(NG):
                        act.activation(hn[:, g * P:(g + 1) * P], z[:, g * P:(g + 1) * P], ACT.Identity,
                                       bias=nmr[:, g:g + 1], scale=rs[:, 1, g:g + 1]).then_inc(sem["hn"], 1)
                if a is not None:
                    mix_out(a, 2)
                if n is not None:
                    wait(act, "x1_tr", n + 1)
                    wait(act, "resid", n - 1)
                    act.activation(x1_tok[:, q, :], dn[3][:, :], ACT.Copy).then_inc(sem["x1_tok"], 1)
                    wait(act, "hn_tr", n + 1)
                    wait(act, "qkv_mm", 3 * n)
                    act.activation(hn_t[:, :], dn[2][:, :], ACT.Identity, bias=col["ln1_b"],
                                   scale=col["ln1_g"]).then_inc(sem["hn_t"], 1)
                if j is not None:
                    wait(act, "pv_mm", j + 1)
                    wait(act, "o_t", j)
                    act.activation(acc[:, :, :], heads_out(0), ACT.Copy,
                                   scale=col["mask_h"][:, 0:1]).then_inc(sem["diag0"], 1)
                    wait(act, "recip", j + 1)
                    wait(act, "rt_mm", j)
                    act.activation(rc[:, :, :], r64[:, :].unsqueeze(2).to_broadcast([P, NG * NH, D]),
                                   ACT.Copy).then_inc(sem["rcx"], 1)
                if a is not None:
                    mix_out(a, 3)
                if n is not None:
                    wait(act, "qkv_mm", 3 * n + 1)
                    wait(act, "s_mm", NI * n)
                    act.activation(qt[:, :], dn[0][:, :], ACT.Identity, bias=col["bq"]).then_inc(sem["q_out"], 1)
                    wait(act, "qkv_mm", 3 * n + 2)
                    wait(act, "pv_mm", n)
                    act.activation(v[:, :, :], groups(dn[3][:, :]), ACT.Copy).then_inc(sem["v_out"], 1)
                if a is not None:
                    wait(act, "y_mm", a + 1)
                    wait(act, "yb2", a)
                    act.activation(yb[:, :], dn[2][:, :], ACT.Copy, scale=s_out[:, 0:1]).then_inc(sem["y_out"], 1)
                if n is not None:
                    wait(act, "qkv_mm", 3 * n + 3)
                    for h in range(HQ):
                        act.activation(kx[:, :, h, :], dn[1][:, :].rearrange("p (b s) -> p b s", s=S), ACT.Identity,
                                       bias=bk_mask[:, h:h + 1], scale=col["mask_h"][:, h:h + 1]).then_inc(sem["kx_out"], 1)

            def between(act):
                act.wait_ge(sem["setup2"], 5)

            act.wait_ge(sem["setup"], 14)
            run(act, iteration, between)
            moe_act(act)

        @block.vector
        def _(dve):
            setup_dve(dve)

            def norm(stats, mean_var, src, signal, count):
                for g in range(NG):
                    dve.bn_stats(stats[:, g, :], src(g)).then_inc(sem[signal], 1)
                wait(dve, signal, 2 * NG * count + NG)
                hold(dve, "held_dve")
                for g in range(NG):
                    dve.bn_aggr(mean_var[:, g, :], stats[:, g, :]).then_inc(sem[signal], 1)

            def pick(m):
                wait(dve, "gate_mm", m + 1)
                dve.tensor_tensor(lg[:, :, :], dn[0][:, 0:NG * E].rearrange("p (g e) -> p g e", e=E),
                                  over_groups(col["gate_b"]), ALU.add).then_inc(sem["pick"], 1)
                wait(dve, "pick", 6 * m + 1)
                dve.tensor_reduce(lmax[:, :], lg[:, :, :], AX.X, ALU.max).then_inc(sem["pick"], 1)
                wait(dve, "pick", 6 * m + 2)
                dve.tensor_tensor(oh[:, :, :], lg[:, :, :], lmax[:, :].unsqueeze(2).to_broadcast([P, NG, E]),
                                  ALU.is_equal).then_inc(sem["pick"], 1)
                wait(dve, "pick", 6 * m + 3)
                dve.tensor_tensor(lg[:, :, :], oh[:, :, :], over_groups(col["rank8"]),
                                  ALU.mult).then_inc(sem["pick"], 1)
                wait(dve, "pick", 6 * m + 4)
                dve.tensor_reduce(lmax[:, :], lg[:, :, :], AX.X, ALU.max).then_inc(sem["pick"], 1)
                wait(dve, "pick", 6 * m + 5)
                dve.tensor_tensor(oh_b[:, :, :], lg[:, :, :], lmax[:, :].unsqueeze(2).to_broadcast([P, NG, E]),
                                  ALU.is_equal).then_inc(sem["pick"], 1)

            def place(m, p):
                q = 1 - p
                wait(dve, "rank_mm", m + 1)
                dve.tensor_tensor(pos[:, :, :], dn[0][:, 64:64 + NG * E].rearrange("p (g e) -> p g e", e=E),
                                  over_groups(base[:, q, :]), ALU.add).then_inc(sem["slot"], 1)
                dve.tensor_tensor(base[:, p, :], dn[0][:, 64 + NG * E:64 + (NG + 1) * E], base[:, q, :],
                                  ALU.add).then_inc(sem["slot"], 1)
                wait(dve, "slot", 5 * m + 2)
                dve.tensor_tensor(pos[:, :, :], pos[:, :, :], oh_b[:, :, :], ALU.mult).then_inc(sem["slot"], 1)
                wait(dve, "slot", 5 * m + 3)
                dve.tensor_reduce(slot_f[:, :], pos[:, :, :], AX.X, ALU.add).then_inc(sem["slot"], 1)
                wait(dve, "slot", 5 * m + 4)
                wait(dve, "scattered", 16 * NG * m)
                dve.tensor_copy(slot[:, :], slot_f[:, :]).then_inc(sem["slot"], 1)

            def shifted(j, blocks):
                for i in blocks:
                    s = so[:, i, :].rearrange("p (n s) -> p n s", s=S)
                    m16 = mx[:, i * NG * HQ:(i + 1) * NG * HQ]
                    wait(dve, "s_mm", NI * j + i + 1)
                    dve.tensor_reduce(m16, s, AX.X, ALU.max).then_inc(sem["smax"], 1)
                    wait(dve, "smax", NI * j + i + 1)
                    wait(dve, "st", NI * j)
                    wait(dve, "sums", 3 * j)
                    dve.tensor_tensor(pr[:, i, :].rearrange("p (n s) -> p n s", s=S), s,
                                      m16.unsqueeze(2).to_broadcast([P, NG * HQ, S]),
                                      ALU.subtract).then_inc(sem["ssub"], 1)

            def turned(j, i):
                wait(dve, "sexp", NI * j + i + 1)
                wait(dve, "pv_mm", j)
                dve.transpose(pt[:, i, :], pr[:, i, :]).then_inc(sem["st"], 1)

            def iteration(a, n, j, m, p):
                q = 1 - p
                if a is not None:
                    wait(dve, "h_mm", a + 1)
                    wait(dve, "u_mm", a)
                    dve.tensor_tensor(hs[:, :].rearrange("p (b s) -> p b s", s=S),
                                      dn[0][:, :].rearrange("p (b s) -> p b s", s=S),
                                      col["lora_w"][:, bass.ds(a * CB, CB)].unsqueeze(2).to_broadcast([P, CB, S]),
                                      ALU.mult).then_inc(sem["hs"], 1)
                if m is not None:
                    wait(dve, "wo_mm", m + 1)
                    wait(dve, "zb", m + 1)
                    wait(dve, "resid", m)
                    wait(dve, "hn2", NG * m)
                    dve.tensor_tensor(xp[:, :], dn[3][:, :], zb[:, q, :], ALU.add).then_inc(sem["xp"], 1)
                    wait(dve, "xp", m + 1)
                    norm(bn2, mv2, lambda g: xp[:, g * P:(g + 1) * P], "ln2", m)
                if j is not None:
                    shifted(j, range(0, 1))
                if m is not None:
                    wait(dve, "rstd2", 2 * (m + 1))
                    dve.scalar_tensor_tensor(nmr2[:, :], mv2[:, :, 0], -1.0, rs2[:, 1, :], ALU.mult,
                                             ALU.mult).then_inc(sem["nmr2"], 1)
                if j is not None:
                    shifted(j, range(1, NI))
                if a is not None:
                    wait(dve, "uv", a + 1)
                    dve.tensor_scalar(magic[:, :].bitcast(U32), uv[:, :].bitcast(U32), 0x7F800000, 0x00400000,
                                      ALU.bitwise_and, ALU.bitwise_or).then_inc(sem["pow2"], 1)
                if n is not None:
                    wait(dve, "z_mm", n + 1)
                    wait(dve, "zb", n)
                    wait(dve, "hn", NG * n)
                    dve.tensor_tensor(groups(z[:, :]), groups(dn[0][:, :]), over_groups(col["mix_bias"]),
                                      ALU.add).then_inc(sem["z"], 1)
                    wait(dve, "z", n + 1)
                    norm(bn, mv, lambda g: z[:, g * P:(g + 1) * P], "ln1", n)
                if j is not None:
                    turned(j, 0)
                    turned(j, 1)
                if n is not None:
                    wait(dve, "rstd1", 2 * (n + 1))
                    dve.scalar_tensor_tensor(nmr[:, :], mv[:, :, 0], -1.0, rs[:, 1, :], ALU.mult,
                                             ALU.mult).then_inc(sem["nmr1"], 1)
                if j is not None:
                    turned(j, 2)
                    turned(j, 3)
                if m is not None:
                    pick(m)
                if a is not None:
                    wait(dve, "pow2", a + 1)
                    wait(dve, "gv", a + 1)
                    dve.scalar_tensor_tensor(gv[:, :], magic[:, :], 1.5 * 2.0 ** -6, gv[:, :], ALU.max,
                                             ALU.add).then_inc(sem["q8"], 1)
                if j is not None:
                    wait(dve, "sums", 3 * (j + 1))
                    dve.tensor_reduce(t1[:, :].rearrange("p (g i h) -> p i g h", g=NG, i=NI),
                                      t4[:, :, :].rearrange("p (i g h) s -> p i g h s", i=NI, g=NG), AX.X,
                                      ALU.add).then_inc(sem["rsum"], 1)
                    wait(dve, "rsum", j + 1)
                    wait(dve, "rcx", j)
                    dve.reciprocal(r64[:, :], t1[:, :]).then_inc(sem["recip"], 1)
                if a is not None:
                    wait(dve, "q8", 2 * a + 1)
                    wait(dve, "y_mm", a)
                    dve.scalar_tensor_tensor(q8[:, :], magic[:, :], 1.5 * 2.0 ** -6, gv[:, :], ALU.max,
                                             ALU.subtract).then_inc(sem["q8"], 1)
                if m is not None:
                    place(m, p)
                if j is not None:
                    wait(dve, "diag0", j + 1)
                    for h in range(1, HQ):
                        dve.scalar_tensor_tensor(acc[:, :, :], heads_out(h), col["mask_h"][:, h:h + 1], acc[:, :, :],
                                                 ALU.mult, ALU.add).then_inc(sem["diag"], 1)
                        wait(dve, "diag", 3 * j + h)
                    wait(dve, "rt_mm", j + 1)
                    wait(dve, "wo_mm", j)
                    dve.tensor_tensor(o_t[:, :, :, :].rearrange("p g b s -> p b g s"),
                                      acc[:, :, :].rearrange("p (b g) s -> p b g s", b=GB),
                                      dn[2][:, :].rearrange("p (g b s) -> p b g s", g=NG, b=GB),
                                      ALU.mult).then_inc(sem["o_t"], 1)
                if a is not None:
                    wait(dve, "y_out", a + 1)
                    wait(dve, "x1", a)
                    dve.tensor_scalar(yb2[:, :], yb[:, :], bias8f[:, 0:1], None, ALU.add).then_inc(sem["yb2"], 1)

            run(dve, iteration, setup2_dve)
            moe_dve(dve)

        @block.gpsimd
        def _(pool):
            pool.memset(minus_half[:, :], -0.5).then_inc(sem["consts"], 1)
            pool.memset(pad[:, 0:2 * H], 0.0).then_inc(sem["consts"], 1)
            pool.memset(pad[:, 2 * H:ROW], PAD_ID).then_inc(sem["consts"], 1)
            pool.memset(ybd[:, :, :], 0.0).then_inc(sem["consts"], 1)
            pool.wait_ge(sem["consts"], 4)

            def rstd(dst, mean_var, signal, source, count):
                wait(pool, source, 2 * NG * (count + 1))
                hold(pool, "held_pool")
                pool.tensor_scalar(dst[:, 0, :], mean_var[:, :, 1], EPS, 1.0, ALU.add, ALU.mult).then_inc(sem[signal], 1)
                wait(pool, signal, 2 * count + 1)
                pool.tensor_tensor(dst[:, 1, :], dst[:, 0, :], minus_half[:, :], ALU.pow).then_inc(sem[signal], 1)

            def iteration(a, n, j, m, p):
                q = 1 - p
                if isinstance(a, int) and a == 0:
                    pool.wait_ge(sem["in1"], 16)
                    pool.tensor_tensor(col["mix_w"], col["mix_w"], col["mix_mask"], ALU.mult).then_inc(sem["mix_masked"], 1)
                if m is not None:
                    rstd(rs2, mv2, "rstd2", "ln2", m)
                    wait(pool, "xp", m + 1)
                    wait(pool, "x1_tok", m + 1)
                    wait(pool, "scattered", 16 * NG * m)
                    hold(pool, "held_pool")
                    pool.tensor_tensor(rows[:, :, H:2 * H], groups(x1_tok[:, q, :]), groups(xp[:, :]),
                                       ALU.add).then_inc(sem["resid"], 1)
                    pool.tensor_copy(rows[:, :, 2 * H], col["ids"][:, bass.ds(m * NG, NG)]).then_inc(sem["ids"], 1)
                if a is not None:
                    wait(pool, "wb_mm", 4 * a)
                    hold(pool, "held_pool")
                    pool.tensor_tensor(ybd[:, :, :],
                                       col["y_rep"][:, bass.ds(a * CB, CB)].unsqueeze(1).to_broadcast([P, 16, CB]),
                                       col["mask_o"].unsqueeze(2).to_broadcast([P, 16, CB]),
                                       ALU.mult).then_inc(sem["ybd"], 1)
                    wait(pool, "uv", a + 1)
                    hold(pool, "held_pool")
                    pool.tensor_scalar(guard[:, :], uv[:, :], F32_MAX / FP8_MAX_IN, 0.0, ALU.mult,
                                       ALU.mult).then_inc(sem["guard"], 1)
                    wait(pool, "guard", a + 1)
                    wait(pool, "uvs", a + 1)
                    wait(pool, "q8", 2 * a)
                    pool.tensor_tensor(gv[:, :], uvs[:, :], guard[:, :], ALU.add).then_inc(sem["gv"], 1)
                if j is not None:
                    e32 = pr[:, :, :].rearrange("p i (n s) -> p (i n) s", s=S)
                    wait(pool, "sexp", NI * (j + 1))
                    pool.tensor_tensor(t16[:, :, :], e32[:, :, 0:16], e32[:, :, 16:32], ALU.add).then_inc(sem["sums"], 1)
                if n is not None:
                    rstd(rs, mv, "rstd1", "ln1", n)
                if j is not None:
                    wait(pool, "sums", 3 * j + 1)
                    pool.tensor_tensor(t8[:, :, :], t16[:, :, 0:8], t16[:, :, 8:16], ALU.add).then_inc(sem["sums"], 1)
                    wait(pool, "sums", 3 * j + 2)
                    wait(pool, "rsum", j)
                    pool.tensor_tensor(t4[:, :, :], t8[:, :, 0:4], t8[:, :, 4:8], ALU.add).then_inc(sem["sums"], 1)
                if n is not None:
                    wait(pool, "z", n + 1)
                    wait(pool, "xp", n - 1)
                    pool.wait_ge(sem["setup2"], 5)
                    pool.tensor_tensor(groups(zb[:, q, :]), groups(z[:, :]), over_groups(bo2[:, :]),
                                       ALU.add).then_inc(sem["zb"], 1)
                if m is not None:
                    wait(pool, "ids", m + 1)
                    wait(pool, "resid", m + 1)
                    wait(pool, "slot", 5 * (m + 1))
                    wait(pool, "hn2", NG * (m + 1))
                    hold(pool, "held_pool")
                    for g in range(NG):
                        pool.indirect_dma_start(routed, bass.IndirectOffsetOnAxis(slot[:, g:g + 1], 0),
                                                rows[:, g, :], None).then_inc(sem["scattered"], 16)
                if a is not None:
                    wait(pool, "yb2", a + 1)
                    wait(pool, "x1_tr", a - 1)
                    pool.tensor_tensor(x1[:, p, :], xb[:, p, :], yb2[:, :], ALU.add).then_inc(sem["x1"], 1)

            run(pool, iteration)
            moe_pool(pool)


def shape_constants():
    p = np.arange(P)
    c = {
        "ident": np.eye(P),
        "mask_o": (p[:, None] // G == np.arange(16)),
        "mask_h": (p[:, None] % 32 // D == np.arange(HQ)),
        "upper": (p[:, None] < p[None, :]),
        "ids": p[:, None] + P * np.arange(N_TOK // P),
        "region": np.broadcast_to(REGION * np.arange(E), (P, E)),
        "rank8": np.broadcast_to(E - np.arange(E), (P, E)),
        "tile_no": np.broadcast_to(np.arange(NT), (P, NT)),
        "expert_no": np.broadcast_to(np.arange(E), (P, E)),
    }
    return {k: np.ascontiguousarray(x, np.float32) for k, x in c.items()}


def kernel(**inputs):
    import concourse.bacc as bacc
    from concourse.bass_utils import run_bass_kernel_spmd

    a = {k: np.asarray(x) for k, x in inputs.items()}

    def rows(x):
        return np.broadcast_to(x.reshape(1, -1), (P, x.size))

    def column(x):
        return x.reshape(P, 1)

    w1 = a["L1_ffn_w1"].transpose(1, 0, 2)
    b1 = a["L1_ffn_b1"].reshape(E, FB, P).transpose(2, 0, 1)
    parts = shape_constants() | {
        "lora_a": a["L0_cond_As"].reshape(P, H).T,
        "w_base": a["L0_cond_W_base"].T,
        "lora_b": a["L0_cond_Bs"].transpose(0, 2, 1).reshape(P, H),
        "lora_w": np.repeat(a["cond_8"].T, R, axis=0),
        "b_base": column(a["L0_cond_b_base"]),
        "s_in": rows(a["L0_ffn_input_scale"]),
        "s_k": rows(a["L0_ffn_kernel_scale"]),
        "y_rep": np.tile(a["cond_8"].T, (16, 1)),
        "mix_w": a["L1_cond_weight"].reshape(G, 8, 16, H).transpose(2, 0, 1, 3).reshape(P, G * H),
        "mix_mask": np.repeat(a["L1_cond_mask"].reshape(8, 16, H).transpose(1, 0, 2), G, axis=0).reshape(P, G * H),
        "wq": a["L1_ffn_wq"], "wk": a["L1_ffn_wk"], "wv": a["L1_ffn_wv"], "wo": a["L1_ffn_wo"],
        "gate_w": a["L1_ffn_gate_w"],
        "ln1_g": column(a["L1_ffn_ln1_g"]), "ln1_b": column(a["L1_ffn_ln1_b"]),
        "ln2_g": column(a["L1_ffn_ln2_g"]), "ln2_b": column(a["L1_ffn_ln2_b"]),
        "bq": column(a["L1_ffn_bq"]), "bk": column(a["L1_ffn_bk"]),
        "mix_bias": rows(a["L1_cond_bias"]), "bv": column(a["L1_ffn_bv"]), "bo": rows(a["L1_ffn_bo"]),
        "gate_b": rows(a["L1_ffn_gate_b"]),
        "w1": np.concatenate([w1, b1], axis=2).reshape(P, E * (F + FB)),
        "w2": a["L1_ffn_w2"].reshape(E, FB, P, H).transpose(2, 0, 1, 3).reshape(P, E * F),
        "b2": rows(a["L1_ffn_b2"]),
    }
    arrays = {f"pack{n}": np.ascontiguousarray(np.concatenate([parts[name] for name, _ in part], axis=1))
              for n, part in enumerate(PACK)}
    arrays["x_t"] = np.ascontiguousarray(a["x"].reshape(N_TOK, H).T)
    arrays["kernel8"] = np.ascontiguousarray(a["L0_ffn_kernel"])
    arrays["bias8"] = np.ascontiguousarray(a["L0_ffn_bias"].reshape(P, 1))

    nc = bacc.Bacc("TRN2", target_bir_lowering=False, num_devices=1)
    dram = {name: nc.dram_tensor(name, x.shape, mybir.dt.from_np(x.dtype), kind="ExternalInput").ap()
            for name, x in arrays.items()}
    out = nc.dram_tensor("out", (N_TOK, H), F32, kind="ExternalOutput").ap()
    build(nc, dram["x_t"], [dram[f"pack{n}"] for n in range(len(PACK))], dram["kernel8"], dram["bias8"], out)
    r = run_bass_kernel_spmd(nc, [arrays], core_ids=[0])
    return np.asarray(r.results[0]["out"]).reshape(B, S, H)
```

```python
from contextlib import ExitStack

import numpy as np

import concourse.bass as bass
from concourse import mybir

F32 = mybir.dt.float32
BF16 = mybir.dt.bfloat16
U32 = mybir.dt.uint32
ALU = mybir.AluOpType
ACT = mybir.ActivationFunctionType
AX = mybir.AxisListType

P = 128
B, S, H = 128, 32, 128
N_TOK = B * S
G = 8
R = 16
LORA_SCALE = 2.0
NH, D = 16, 8
E, F = 8, 512
EPS = 1e-5
CHUNK = 512
NC = N_TOK // CHUNK
CB = CHUNK // S
NG = CHUNK // P
GB = P // S
HQ = 4
NI = H // 32
FB = F // P
ROW = 2 * H + 1
REGION = N_TOK + P
NT = (N_TOK + E * (P - 1)) // P
NF = -(-NT // 4)
PAD_ID = 65536.0
FP8_MAX_IN = 464.0
F32_MAX = 3.4028234e38
MIX_BANK = (1, 2, 1, 3)
SCHED_STEPS = 20
SETUP_STEPS = 13
W1_WIDTH = F + FB + H

PACK = [
    [("lora_a", H), ("w_base", H), ("lora_b", H), ("lora_w", B), ("b_base", 1), ("s_in", 1), ("s_k", 1)],
    [("mask_o", 16), ("y_rep", B), ("mix_w", G * H), ("mix_mask", G * H)],
    [("ident", P), ("wq", H), ("wk", H), ("wv", H), ("wo", H), ("gate_w", E), ("ln1_g", 1), ("ln1_b", 1),
     ("ln2_g", 1), ("ln2_b", 1), ("bq", 1), ("bk", 1), ("mask_h", HQ), ("mix_bias", H), ("bv", 1), ("bo", H),
     ("gate_b", E), ("upper", P), ("ids", N_TOK // P), ("region", E), ("rank8", E), ("tile_no", 1),
     ("tile_at", 1), ("expert_no", E), ("octal", 4 * NF)],
    [("w1", E * W1_WIDTH), ("w2", E * F)],
]
WIDTH = [sum(w for _, w in part) for part in PACK]


def build(nc, x_t, packs, kernel8, bias8, out):
    ctx = ExitStack()
    with ctx:
        def sb(name, shape, dt=F32):
            return ctx.enter_context(nc.sbuf_tensor(name, shape, dt))

        names = """in0 in1 in2 in3 in8 consts mix_masked setup setup2 bias8_out bias_mm x_in0 x_in1
            h_mm hs u_mm u_out uv uvs pow2 guard gv q8 y_mm y_out yb2 x1 ybd wb_mm wb_out
            z_mm x1_tr x1_tok z ln1 rstd1 nmr1 hn hn_tr hn_t qkv_mm q_out kx_out v_out zb
            s_mm smax ssub sexp st sums rsum recip rcx pv_mm rt_mm diag0 diag o_t
            wo_mm xp ln2 rstd2 nmr2 hn2 resid tr2 hn2_t gate_mm pick rank_mm ids slot scattered
            sched pads rows_in0 rows_in1 rows_in2 rows_in3 w1_staged t_tr t_xt mid_mm relu_a relu_v out_mm
            tiles_tr res fin stored0 stored1 stored2 stored3 held_pe held_dve held_pool""".split()
        sem = {n: ctx.enter_context(nc.semaphore(n)) for n in names}

        def wait(eng, name, value):
            if isinstance(value, int) and value <= 0:
                return
            eng.wait_ge(sem[name], value)

        def wait_turn(eng, name, s, u, turns):
            wait(eng, f"{name}{u}", (16 // turns) * (s - u) + 16)

        def hold(eng, name):
            eng.sem_inc(sem[name], 1)

        pk = [sb(f"pack{n}_sb", [P, w]) for n, w in enumerate(WIDTH)]
        col = {}
        for n, part in enumerate(PACK):
            at = 0
            for name, w in part:
                col[name] = pk[n][:, at:at + w]
                at += w
        k8_in = sb("k8_in", [P, H], BF16)
        bias8_in = sb("bias8_in", [P, 1], BF16)
        k8f = sb("k8f", [P, H])
        k8_magic = sb("k8_magic", [P, H])
        k8_guard = sb("k8_guard", [P, H])
        k8 = sb("k8", [P, H], BF16)
        bias8f = sb("bias8f", [P, 1])
        r_in = sb("r_in", [P, 1])
        r_k = sb("r_k", [P, 1])
        s_out = sb("s_out", [P, 1])
        bk_mask = sb("bk_mask", [P, HQ])
        minus_half = sb("minus_half", [P, NG])
        ones_b = sb("ones_b", [P, P], BF16)
        upper_b = sb("upper_b", [P, P], BF16)
        pad = sb("pad", [P, ROW])
        base = sb("base", [P, 2, E])

        xb = sb("xb", [P, 2, CHUNK])
        hs = sb("hs", [P, CHUNK])
        ub = sb("ub", [P, CHUNK], BF16)
        uv = sb("uv", [P, CHUNK])
        uvs = sb("uvs", [P, CHUNK])
        magic = sb("magic", [P, CHUNK])
        guard = sb("guard", [P, CHUNK])
        gv = sb("gv", [P, CHUNK])
        x1_tok = sb("x1_tok", [P, 2, CHUNK])
        nmr = sb("nmr", [P, NG])
        nmr2 = sb("nmr2", [P, NG])
        r_in20 = sb("r_in20", [P, 1])
        bv_b = sb("bv_b", [P, H])
        bo2 = sb("bo2", [P, H])
        r64 = sb("r64", [P, NG * NH])
        q8 = sb("q8", [P, CHUNK], BF16)
        yb = sb("yb", [P, CHUNK], BF16)
        yb2 = sb("yb2", [P, CHUNK], BF16)
        x1 = sb("x1", [P, 2, CHUNK])
        ybd = sb("ybd", [P, 16, CB])
        wb = sb("wb", [P, CB, H])
        z = sb("z", [P, CHUNK])
        zb = sb("zb", [P, 2, CHUNK])
        bn = sb("bn", [P, NG, 6])
        mv = sb("mv", [P, NG, 2])
        rs = sb("rs", [P, 2, NG])
        hn = sb("hn", [P, CHUNK])
        hn_t = sb("hn_t", [P, CHUNK])
        qt = sb("qt", [P, CHUNK])
        kx = sb("kx", [P, CB, HQ, S])
        v = sb("v", [P, NG, H])
        mx = sb("mx", [P, NI * NG * HQ])
        pr = sb("pr", [P, NI, NG * HQ * S])
        pt = sb("pt", [P, NI, NG * HQ * S])
        t16 = sb("t16", [P, 64, 16])
        t8 = sb("t8", [P, 64, 8])
        t4 = sb("t4", [P, 64, 4])
        t1 = sb("t1", [P, 64])
        rc = sb("rc", [P, NG * NH, D])
        acc = sb("acc", [P, GB * NG, S])
        o_t = sb("o_t", [P, NG, GB, S])
        xp = sb("xp", [P, CHUNK])
        bn2 = sb("bn2", [P, NG, 6])
        mv2 = sb("mv2", [P, NG, 2])
        rs2 = sb("rs2", [P, 2, NG])
        rows = sb("rows", [P, NG, ROW])
        hn2_t = sb("hn2_t", [P, CHUNK])
        lg = sb("lg", [P, NG, E])
        lmax = sb("lmax", [P, NG])
        oh = sb("oh", [P, NG, E])
        oh_b = sb("oh_b", [P, NG, E], BF16)
        pos = sb("pos", [P, NG, E])
        slot_f = sb("slot_f", [P, NG])
        slot = sb("slot", [P, NG], U32)

        sched = {n: sb(f"sched_{n}", shape) for n, shape in dict(
            n=[P, E], c0=[P, 2 * E], c1=[P, 2 * E], c2=[P, 2 * E], c3=[P, 2 * E], off=[P, E], le=[P, E],
            none=[P, 1], of=[P, 2, E], pair=[P, 2], octal=[1, 4 * NF], fours=[1, NF + 1],
            eights=[1, NF]).items()}
        sched["in"] = sb("sched_in", [P, E])
        count_u = sb("count_u", [P, E], U32)
        pad_row = sb("pad_row", [1, E], U32)
        rows_u = sb("rows_u", [1, NT], U32)
        eights_u = sb("eights_u", [1, NF], U32)
        rin = [sb(f"rin{n}", [P, ROW]) for n in range(4)]
        xt = [sb(f"xt{n}", [P, P]) for n in range(2)]
        w1s = [sb(f"w1s{n}", [P, W1_WIDTH]) for n in range(4)]
        mid = [sb(f"mid{n}", [P, FB, P]) for n in range(2)]
        res = [sb(f"res{n}", [P, H]) for n in range(4)]
        ob = [sb(f"ob{n}", [P, H]) for n in range(4)]
        id_u = [sb(f"id_u{n}", [P, 1], U32) for n in range(4)]

        so = ctx.enter_context(nc.psum_tensor("so", [P, 4, 512], F32))
        dn = [ctx.enter_context(nc.psum_tensor(f"d{n}", [P, 512], F32)) for n in range(4)]

        routed = nc.dram_tensor("routed", [(E + 1) * REGION, ROW], F32).ap()

        def groups(ap):
            return ap.rearrange("p (g n) -> p g n", g=NG)

        def over_groups(ap):
            return ap.unsqueeze(1).to_broadcast([P, NG, ap.shape[1]])

        def heads_out(h):
            return so[:, :, :].rearrange("p b (g h s) -> p (b g) h s", g=NG, h=HQ)[:, :, h, :]

        def setup_dve(dve):
            done = sem["setup"]
            dve.memset(ones_b[:, :], 1.0).then_inc(done, 1)
            dve.wait_ge(sem["in0"], 16)
            dve.reciprocal(r_in[:, :], col["s_in"]).then_inc(done, 1)
            dve.reciprocal(r_k[:, :], col["s_k"]).then_inc(done, 1)
            dve.scalar_tensor_tensor(s_out[:, :], col["s_in"], -(2.0 ** 20), col["s_k"], ALU.mult,
                                     ALU.mult).then_inc(done, 1)
            dve.tensor_scalar(col["lora_w"], col["lora_w"], LORA_SCALE, None, ALU.mult).then_inc(done, 1)
            dve.wait_ge(done, 5)
            dve.tensor_scalar(r_in20[:, :], r_in[:, :], 2.0 ** -20, None, ALU.mult).then_inc(done, 1)
            dve.wait_ge(done, 6)

        def setup_k8_dve(dve):
            done = sem["setup"]
            dve.wait_ge(sem["in8"], 32)
            dve.tensor_scalar(k8f[:, :], k8_in[:, :], r_k[:, 0:1], None, ALU.mult).then_inc(done, 1)
            dve.wait_ge(done, 7)
            dve.tensor_scalar(k8_magic[:, :].bitcast(U32), k8f[:, :].bitcast(U32), 0x7F800000, None,
                              ALU.bitwise_and).then_inc(done, 1)
            dve.tensor_scalar(k8_guard[:, :], k8f[:, :], F32_MAX / FP8_MAX_IN, 0.0, ALU.mult,
                              ALU.mult).then_inc(done, 1)
            dve.wait_ge(done, 9)
            dve.tensor_scalar(k8_magic[:, :], k8_magic[:, :], 2.0 ** -6, 1.5 * 2.0 ** 20, ALU.max,
                              ALU.mult).then_inc(done, 1)
            dve.wait_ge(done, 10)
            dve.tensor_tensor(k8_magic[:, :], k8_magic[:, :], k8_guard[:, :], ALU.add).then_inc(done, 1)
            dve.wait_ge(done, 11)
            dve.tensor_tensor(k8f[:, :], k8f[:, :], k8_magic[:, :], ALU.add).then_inc(done, 1)
            dve.wait_ge(done, 12)
            dve.tensor_tensor(k8[:, :], k8f[:, :], k8_magic[:, :], ALU.subtract).then_inc(done, 1)
            dve.wait_ge(done, 13)

        def setup2_dve(dve):
            done = sem["setup2"]
            dve.wait_ge(sem["in2"], 16)
            dve.tensor_scalar(bv_b[:, :], ones_b[:, :], col["bv"], None, ALU.mult).then_inc(done, 1)
            dve.tensor_scalar(bk_mask[:, :], col["mask_h"], col["bk"], None, ALU.mult).then_inc(done, 1)
            dve.tensor_copy(upper_b[:, :], col["upper"]).then_inc(done, 1)
            dve.tensor_copy(base[:, 0, :], col["region"]).then_inc(done, 1)
            dve.wait_ge(sem["bias_mm"], 1)
            dve.tensor_tensor(bo2[:, :], dn[3][:, 0:H], col["bo"], ALU.add).then_inc(done, 1)

        def tiles(eng, step, every=0):
            def four(s, i, place=0, experts=None, count=4):
                if every and experts is None:
                    experts = eight_experts(eng, i)
                for u in range(count):
                    step(s + u, u, *((experts, place + u) if every else ()))
                return experts

            four(0, 0)
            with eng.Fori(0, (NF - 2) // 2) as i:
                experts = four(8 * i + 4, 2 * i + 1)
                four(8 * i + 8, 2 * i + 2, *((4, experts) if every == 8 else ()))
            four(4 * NF - 4, NF - 1, count=NT - 4 * NF + 4)

        def eight_experts(eng, i):
            return eng.value_load(eights_u[0:1, bass.ds(i, 1)], min_val=0, max_val=2 ** 24 - 1)

        def expert(eight, k):
            return (eight >> (3 * k)) & 7

        def last(s, ahead):
            return isinstance(s, int) and s + ahead >= NT

        def pad_rows(eng, experts):
            eng.wait_ge(sem["consts"], 9)
            eng.wait_ge(sem["sched"], 1)
            for e in experts:
                row = eng.value_load(pad_row[0:1, e:e + 1], min_val=0, max_val=E * REGION)
                eng.dma_start(routed[bass.ds(row, P), :], pad[:, :]).then_inc(sem["pads"], 16)

        def moe_sp(sp):
            pad_rows(sp, range(0, E // 2))
            sp.wait_ge(sem["sched"], SCHED_STEPS - 4)
            sp.wait_ge(sem["pads"], 16 * (E + 1))
            sp.wait_ge(sem["scattered"], 16 * NG * NC)

            def step(s, u):
                row = sp.value_load(rows_u[0:1, bass.ds(s, 1)], min_val=0, max_val=E * REGION)
                wait(sp, "res", 2 * (s - 3))
                sp.dma_start(rin[u][:, :], routed[bass.ds(row, P), :]).then_inc(sem[f"rows_in{u}"], 16)

            tiles(sp, step)

        def moe_pe(pe):
            def turn(s, u):
                wait_turn(pe, "rows_in", s, u, 4)
                wait(pe, "t_xt", s - 1)
                pe.transpose(dn[u % 2][:, 0:P], rin[u][:, 0:H], col["ident"]).then_inc(sem["t_tr"], 1)

            def hidden(s, u):
                wait(pe, "t_xt", s + 1)
                wait(pe, "w1_staged", s + 1)
                wait(pe, "relu_a", 3 * (s - 1))
                wait(pe, "relu_v", s - 1)
                for k in range(FB):
                    mm = pe.matmul(so[:, 2 * (k // 3) + u % 2, (k % 3) * P:(k % 3 + 1) * P],
                                   w1s[u][:, k * P:(k + 1) * P], xt[u % 2][:, :], start=True, stop=True)
                mm.then_inc(sem["mid_mm"], 1)

            def output(s, u, e):
                wait(pe, "relu_a", 3 * (s + 1))
                wait(pe, "relu_v", s + 1)
                wait(pe, "fin", s - 1)
                for k in range(FB):
                    mm = pe.matmul(dn[2 + u % 2][:, 0:H], mid[u % 2][:, k, :],
                                   col["w2"][:, bass.ds(e * F + k * H, H)], start=(k == 0), stop=(k == FB - 1))
                mm.then_inc(sem["out_mm"], 1)

            def step(s, u, experts, place):
                e = expert(experts, place)
                if not last(s, 1):
                    hidden(s + 1, (u + 1) % 4)
                if not last(s, 2):
                    turn(s + 2, (u + 2) % 4)
                output(s, u, e)

            pe.wait_ge(sem["slot"], 5 * NC)
            pe.wait_ge(sem["resid"], NC)
            pe.wait_ge(sem["o_t"], NC)
            pe.wait_ge(sem["hn2_t"], NC)
            pe.wait_ge(sem["sched"], SCHED_STEPS - 5)
            for k in range(2):
                mm = pe.transpose(dn[0][0:1, k * P:(k + 1) * P], sched["pair"][:, k:k + 1], col["ident"])
            mm.then_inc(sem["tiles_tr"], 1)
            pe.wait_ge(sem["sched"], SCHED_STEPS)
            turn(0, 0)
            hidden(0, 0)
            turn(1, 1)
            tiles(pe, step, 8)

        def moe_act(act):
            def normed(s, u):
                wait(act, "t_tr", s + 1)
                wait(act, "mid_mm", s - 1)
                act.activation(xt[u % 2][:, :], dn[u % 2][:, 0:P], ACT.Identity, bias=col["ln2_b"],
                               scale=col["ln2_g"]).then_inc(sem["t_xt"], 1)

            def relu(s, u):
                wait(act, "mid_mm", s + 1)
                wait(act, "out_mm", s - 1)
                for k in range(3):
                    act.activation(mid[u % 2][:, k, :], so[:, u % 2, k * P:(k + 1) * P], ACT.Relu,
                                   bias=w1s[u][:, F + k:F + k + 1]).then_inc(sem["relu_a"], 1)

            def step(s, u):
                if not last(s, 2):
                    normed(s + 2, (u + 2) % 4)
                if not last(s, 1):
                    relu(s + 1, (u + 1) % 4)

            pad_rows(act, range(E // 2, E))
            normed(0, 0)
            normed(1, 1)
            relu(0, 0)
            tiles(act, step)

        def moe_dve(dve):
            count = [0]

            def link(ins, ends=True):
                count[0] += 1
                ins.then_inc(sem["sched"], 1)
                if ends:
                    dve.wait_ge(sem["sched"], count[0])

            t = sched
            tile_no, tile_at = col["tile_no"], col["tile_at"]
            before, after = t["c3"][:, E - 1:2 * E - 1], t["c3"][:, E:2 * E]
            dve.wait_ge(sem["slot"], 5 * NC)
            dve.wait_ge(sem["consts"], 9)
            link(dve.tensor_copy(pad_row[:, :], base[0:1, 0, :]), False)
            link(dve.tensor_tensor(t["n"][:, :], base[:, 0, :], col["region"], ALU.subtract))
            link(dve.tensor_scalar(count_u[:, :], t["n"][:, :], 1.0 / P, (P - 1) / P - 0.5 + 0.5 / P, ALU.mult, ALU.add))
            link(dve.tensor_copy(t["c0"][:, E:2 * E], count_u[:, :]))
            for n in range(3):
                a, b = t[f"c{n}"], t[f"c{n + 1}"]
                link(dve.tensor_tensor(b[:, E:2 * E], a[:, E:2 * E], a[:, E - 2 ** n:2 * E - 2 ** n], ALU.add))
            link(dve.scalar_tensor_tensor(t["off"][:, :], before, -float(P), col["region"], ALU.mult, ALU.add), False)
            link(dve.tensor_scalar(t["none"][:, :], after[:, E - 1:E], tile_no, float(E * REGION), ALU.is_le,
                                   ALU.mult), False)
            link(dve.tensor_scalar(t["le"][:, :], before, tile_no, None, ALU.is_le))
            link(dve.scalar_tensor_tensor(t["in"][:, :], after, tile_no, t["le"][:, :], ALU.is_gt, ALU.mult))
            link(dve.scalar_tensor_tensor(t["of"][:, 0, :], t["off"][:, :], tile_at, t["in"][:, :], ALU.add,
                                          ALU.mult), False)
            link(dve.tensor_tensor(t["of"][:, 1, :], t["in"][:, :], col["expert_no"], ALU.mult))
            link(dve.tensor_reduce(t["pair"][:, :], t["of"][:, :, :], AX.X, ALU.add))
            link(dve.tensor_tensor(t["pair"][:, 0:1], t["pair"][:, 0:1], t["none"][:, :], ALU.add))
            dve.wait_ge(sem["tiles_tr"], 1)
            link(dve.tensor_copy(rows_u[:, :], dn[0][0:1, 0:NT]), False)
            link(dve.tensor_tensor(t["octal"][:, :], dn[0][0:1, P:P + 4 * NF], col["octal"][0:1, :], ALU.mult))
            link(dve.tensor_reduce(t["fours"][:, 0:NF], t["octal"][:, :].rearrange("p (i k) -> p i k", k=4), AX.X,
                                   ALU.add))
            link(dve.scalar_tensor_tensor(t["eights"][:, :], t["fours"][:, 1:NF + 1], 8.0 ** 4,
                                          t["fours"][:, 0:NF], ALU.mult, ALU.add))
            link(dve.tensor_copy(eights_u[:, :], t["eights"][:, :]))
            assert count[0] == SCHED_STEPS

            def relu(s, u):
                wait(dve, "mid_mm", s + 1)
                wait(dve, "out_mm", s - 1)
                dve.tensor_scalar(mid[u % 2][:, 3, :], so[:, 2 + u % 2, 0:P], w1s[u][:, F + 3:F + 4], 0.0,
                                  ALU.add, ALU.max).then_inc(sem["relu_v"], 1)

            def finish(s, u):
                wait(dve, f"stored{u}", 4 * (s - u))
                wait(dve, "res", 2 * s + 1)
                wait(dve, "out_mm", s + 1)
                dve.tensor_tensor(ob[u][:, :], dn[2 + u % 2][:, 0:H], res[u][:, :], ALU.add).then_inc(sem["fin"], 1)

            def stage(s, u, e):
                wait(dve, "mid_mm", s - 3)
                wait(dve, "relu_a", 3 * (s - 3))
                wait(dve, "relu_v", s - 3)
                wait(dve, "res", 2 * (s - 3))
                dve.tensor_copy(w1s[u][:, :], col["w1"][:, bass.ds(e * W1_WIDTH, W1_WIDTH)]).then_inc(sem["w1_staged"], 1)

            def step(s, u, experts, place):
                if not last(s, 1):
                    relu(s + 1, (u + 1) % 4)
                finish(s, u)
                if not last(s, 3):
                    stage(s + 3, (u + 3) % 4, expert(experts, place + 3))

            dve.wait_ge(sem["in3"], 16)
            experts = eight_experts(dve, 0)
            for s in range(3):
                stage(s, s, expert(experts, s))
            relu(0, 0)
            tiles(dve, step, 4)

        def moe_pool(pool):
            def residual(s, u):
                wait_turn(pool, "rows_in", s, u, 4)
                wait(pool, "t_tr", s + 1)
                wait(pool, "w1_staged", s + 1)
                wait(pool, "fin", s - 3)
                wait(pool, f"stored{u}", 4 * (s - u))
                hold(pool, "held_pool")
                pool.tensor_tensor(res[u][:, :], rin[u][:, H:2 * H], w1s[u][:, F + FB:], ALU.add).then_inc(sem["res"], 1)
                pool.tensor_copy(id_u[u][:, :], rin[u][:, 2 * H:ROW]).then_inc(sem["res"], 1)

            def step(s, u):
                if not last(s, 1):
                    residual(s + 1, (u + 1) % 4)
                wait(pool, "res", 2 * (s + 1))
                wait(pool, "fin", s + 1)
                hold(pool, "held_pool")
                pool.indirect_dma_start(out, bass.IndirectOffsetOnAxis(id_u[u][:, 0:1], 0), ob[u][:, :], None,
                                        bounds_check=N_TOK - 1, oob_is_err=False).then_inc(sem[f"stored{u}"], 16)

            residual(0, 0)
            tiles(pool, step)
            for u in range(4):
                pool.wait_ge(sem[f"stored{u}"], 16 * ((NT - u + 3) // 4))

        block = ctx.enter_context(nc.Block())

        def run(eng, iteration, between=None):
            iteration(0, None, None, None, 0)
            if between:
                between(eng)
            iteration(1, 0, None, None, 1)
            iteration(2, 1, 0, None, 0)
            loops = (NC - 3) // 2
            with eng.Fori(0, loops) as i:
                for u in range(2):
                    m = 2 * i + u
                    iteration(m + 3, m + 2, m + 1, m, (u + 1) % 2)
            for m in range(2 * loops, NC):
                iteration(*(c if c < NC else None for c in (m + 3, m + 2, m + 1)), m, (m + 1) % 2)

        @block.sync
        def _(sp):
            sp.dma_start(pk[0][:, :], packs[0]).then_inc(sem["in0"], 16)
            sp.dma_start(k8_in[:, :], kernel8).then_inc(sem["in8"], 16)
            sp.dma_start(bias8_in[:, :], bias8).then_inc(sem["in8"], 16)

            def iteration(a, n, j, m, p):
                if a is not None:
                    wait(sp, "x1", a - 1)
                    sp.dma_start(xb[:, p, :], x_t[:, bass.ds(a * CHUNK, CHUNK)]).then_inc(sem[f"x_in{p}"], 16)
                if isinstance(a, int) and a < 3:
                    sp.dma_start(pk[a + 1][:, :], packs[a + 1]).then_inc(sem[f"in{a + 1}"], 16)

            run(sp, iteration)
            sp.wait_ge(sem["consts"], 9)
            sp.dma_start(routed[E * REGION:E * REGION + P, :], pad[:, :]).then_inc(sem["pads"], 16)
            moe_sp(sp)

        @block.tensor
        def _(pe):
            def mix(a, k):
                for u in range(2):
                    blk = 2 * k + u
                    mm = pe.matmul(dn[MIX_BANK[k]][:, u * 256:(u + 1) * 256], col["mix_w"][:, blk * P:(blk + 1) * P],
                                   ybd[:, :, :].rearrange("p o b -> p (o b)"), start=True, stop=True)
                mm.then_inc(sem["wb_mm"], 1)

            def scores(blocks):
                for i in blocks:
                    f = slice(32 * i, 32 * i + 32)
                    for g in range(NG):
                        for b in range(GB):
                            mm = pe.matmul(so[32 * b:32 * b + 32, i, g * P:(g + 1) * P],
                                           qt[f, (g * GB + b) * S:(g * GB + b + 1) * S],
                                           kx[f, g * GB + b, :, :].rearrange("p h s -> p (h s)"),
                                           start=True, stop=True, tile_position=(32 * i, 32 * b))
                    mm.then_inc(sem["s_mm"], 1)

            def values(groups_of):
                for g in groups_of:
                    for b in range(GB):
                        f = slice(32 * b, 32 * b + 32)
                        for i in range(NI):
                            mm = pe.matmul(so[32 * i:32 * i + 32, b, g * P:(g + 1) * P],
                                           v[f, g, 32 * i:32 * i + 32], pt[f, i, g * P:(g + 1) * P],
                                           start=True, stop=True, tile_position=(32 * b, 32 * i))
                return mm

            def iteration(a, n, j, m, p):
                q = 1 - p
                if a is not None:
                    wait_turn(pe, "x_in", a, p, 2)
                    wait(pe, "q_out", a - 1)
                    pe.matmul(dn[0][:, :], col["lora_a"], xb[:, p, :], start=True, stop=True).then_inc(sem["h_mm"], 1)
                    wait(pe, "y_out", a)
                    pe.matmul(dn[2][:, :], col["w_base"], xb[:, p, :], start=True, stop=False)
                    wait(pe, "hs", a + 1)
                    pe.matmul(dn[2][:, :], col["lora_b"], hs[:, :], start=False, stop=True).then_inc(sem["u_mm"], 1)
                if isinstance(a, int) and a == 0:
                    pe.wait_ge(sem["setup2"], 1)
                    pe.matmul(dn[3][:, 0:H], bv_b[:, :], col["wo"], start=True, stop=True).then_inc(sem["bias_mm"], 1)
                if m is not None:
                    wait(pe, "o_t", m + 1)
                    wait(pe, "v_out", m + 2 if not isinstance(m, int) else min(m + 2, NC))
                    wait(pe, "hn2_t", m)
                    for g in range(NG):
                        mm = pe.matmul(dn[3][:, g * P:(g + 1) * P], o_t[:, g, :, :].rearrange("p b s -> p (b s)"),
                                       col["wo"], start=True, stop=True)
                    mm.then_inc(sem["wo_mm"], 1)
                if j is not None:
                    wait(pe, "o_t", j)
                    wait(pe, "q_out", j + 1)
                    wait(pe, "kx_out", HQ * (j + 1))
                    hold(pe, "held_pe")
                    scores(range(0, 2))
                if a is not None:
                    wait(pe, "ybd", a + 1)
                    wait(pe, "wb_out", 4 * a)
                    if m is not None:
                        wait(pe, "o_t", m + 1)
                    pe.wait_ge(sem["mix_masked"], 1)
                    mix(a, 0)
                if n is not None:
                    wait(pe, "x1", n + 1)
                    wait(pe, "wb_out", 4 * (n + 1))
                    wait(pe, "hs", a + 1 if a is not None else NC)
                    wait(pe, "q_out", n)
                    for g in range(NG):
                        for b in range(GB):
                            c = g * GB + b
                            mm = pe.matmul(dn[0][32 * b:32 * b + 32, g * P:(g + 1) * P],
                                           x1[:, q, c * S:(c + 1) * S], wb[:, c, :], start=True, stop=True)
                    mm.then_inc(sem["z_mm"], 1)
                if j is not None:
                    scores(range(2, 3))
                if m is not None:
                    wait(pe, "hn2", NG * (m + 1))
                    wait(pe, "xp", m + 1)
                    for g in range(NG):
                        mm = pe.transpose(dn[3][:, g * P:(g + 1) * P], rows[:, g, 0:H], col["ident"])
                    mm.then_inc(sem["tr2"], 1)
                if j is not None:
                    scores(range(3, NI))
                if a is not None:
                    wait(pe, "u_out", a + 1)
                    mix(a, 1)
                    wait(pe, "wb_out", 4 * a + 1)
                    mix(a, 2)
                    if m is not None:
                        wait(pe, "hn2_t", m + 1)
                    elif n is not None:
                        wait(pe, "v_out", n)
                    else:
                        pe.wait_ge(sem["setup2"], 5)
                    mix(a, 3)
                if m is not None:
                    wait(pe, "hn2_t", m + 1)
                    if n is not None:
                        wait(pe, "z", n + 1)
                    else:
                        wait(pe, "q_out", NC)
                        wait(pe, "slot", 5 * m)
                    for g in range(NG):
                        mm = pe.matmul(dn[0][:, g * E:(g + 1) * E], hn2_t[:, g * P:(g + 1) * P], col["gate_w"],
                                       start=True, stop=True)
                    mm.then_inc(sem["gate_mm"], 1)
                if j is not None:
                    wait(pe, "st", NI * (j + 1))
                    hold(pe, "held_pe")
                    values(range(0, 1))
                if n is not None:
                    wait(pe, "hn", NG * (n + 1))
                    wait(pe, "wb_out", 4 * a + 2 if a is not None else 4 * NC)
                    wait(pe, "y_out", a if a is not None else NC)
                    for g in range(NG):
                        mm = pe.transpose(dn[2][:, g * P:(g + 1) * P], hn[:, g * P:(g + 1) * P], col["ident"])
                    mm.then_inc(sem["hn_tr"], 1)
                if j is not None:
                    values(range(1, 2))
                if n is not None:
                    wait(pe, "wb_out", 4 * a + 4 if a is not None else 4 * NC)
                    wait(pe, "v_out", n)
                    if m is not None:
                        wait(pe, "hn2_t", m + 1)
                    for g in range(NG):
                        mm = pe.transpose(dn[3][:, g * P:(g + 1) * P], x1[:, q, g * P:(g + 1) * P], col["ident"])
                    mm.then_inc(sem["x1_tr"], 1)
                    wait(pe, "hn_t", n + 1)
                    pe.matmul(dn[1][:, :], col["wk"], hn_t[:, :], start=True, stop=True).then_inc(sem["qkv_mm"], 1)
                if m is not None:
                    wait(pe, "pick", 6 * (m + 1))
                    pe.matmul(dn[0][:, 64:64 + NG * E], upper_b[:, :], oh_b[:, :, :].rearrange("p g e -> p (g e)"),
                              start=True, stop=False, skip_group_check=True)
                    for g in range(NG):
                        mm = pe.matmul(dn[0][:, 64 + (g + 1) * E:64 + (NG + 1) * E].rearrange("p (g e) -> p g e", e=E),
                                       ones_b[:, :], oh_b[:, g, :].unsqueeze(1).to_broadcast([P, NG - g, E]),
                                       start=False, stop=(g == NG - 1), skip_group_check=True)
                    mm.then_inc(sem["rank_mm"], 1)
                if j is not None:
                    values(range(2, 3))
                if n is not None:
                    if m is not None:
                        wait(pe, "slot", 5 * m + 2)
                    pe.matmul(dn[0][:, :], col["wq"], hn_t[:, :], start=True, stop=True).then_inc(sem["qkv_mm"], 1)
                if a is not None:
                    wait(pe, "q8", 2 * (a + 1))
                    wait(pe, "wb_out", 4 * a + 2)
                    if n is not None:
                        wait(pe, "hn_t", n + 1)
                    if isinstance(a, int) and a == 0:
                        pe.wait_ge(sem["setup"], SETUP_STEPS)
                    pe.matmul(dn[2][:, :], k8[:, :], q8[:, :], start=True, stop=True).then_inc(sem["y_mm"], 1)
                if j is not None:
                    values(range(3, NG)).then_inc(sem["pv_mm"], 1)
                if n is not None:
                    wait(pe, "x1_tok", n + 1)
                    for g in range(NG):
                        mm = pe.matmul(dn[3][:, g * P:(g + 1) * P], hn_t[:, g * P:(g + 1) * P], col["wv"],
                                       start=True, stop=True)
                    mm.then_inc(sem["qkv_mm"], 1)
                if j is not None:
                    wait(pe, "rcx", j + 1)
                    wait(pe, "kx_out", HQ * (n + 1) if n is not None else HQ * NC)
                    for g in range(NG):
                        mm = pe.transpose(dn[1][:, g * P:(g + 1) * P],
                                          rc[:, g * NH:(g + 1) * NH, :].rearrange("p h d -> p (h d)"), col["ident"])
                    mm.then_inc(sem["rt_mm"], 1)

            pe.wait_ge(sem["in0"], 16)
            run(pe, iteration)
            moe_pe(pe)

        @block.scalar
        def _(act):
            def exponentials(j, blocks):
                for i in blocks:
                    wait(act, "ssub", NI * j + i + 1)
                    act.activation(pr[:, i, :], pr[:, i, :], ACT.Exp, scale=float(D) ** -0.5).then_inc(sem["sexp"], 1)

            def mix_out(a, k):
                wait(act, "wb_mm", 4 * a + k + 1)
                wait(act, "z_mm", a)
                act.activation(wb[:, :, 32 * k:32 * k + 32].rearrange("p b (u o) -> p b u o", u=2),
                               dn[MIX_BANK[k]][:, :].rearrange("p (u o b) -> p b u o", u=2, o=16),
                               ACT.Copy).then_inc(sem["wb_out"], 1)

            def iteration(a, n, j, m, p):
                q = 1 - p
                if a is not None:
                    wait(act, "u_mm", a + 1)
                    act.activation(ub[:, :], dn[2][:, :], ACT.Identity, bias=col["b_base"]).then_inc(sem["u_out"], 1)
                    wait(act, "u_out", a + 1)
                    wait(act, "pow2", a)
                    wait(act, "guard", a)
                    act.activation(uv[:, :], ub[:, :], ACT.Copy, scale=r_in[:, 0:1]).then_inc(sem["uv"], 1)
                    wait(act, "gv", a)
                    act.activation(uvs[:, :], ub[:, :], ACT.Copy, scale=r_in20[:, 0:1]).then_inc(sem["uvs"], 1)
                if j is not None:
                    exponentials(j, range(0, 1))
                if m is not None:
                    wait(act, "nmr2", m + 1)
                    wait(act, "scattered", 16 * NG * m)
                    for g in range(NG):
                        act.activation(rows[:, g, 0:H], xp[:, g * P:(g + 1) * P], ACT.Identity,
                                       bias=nmr2[:, g:g + 1], scale=rs2[:, 1, g:g + 1]).then_inc(sem["hn2"], 1)
                if j is not None:
                    exponentials(j, range(1, 2))
                if a is not None:
                    mix_out(a, 0)
                if j is not None:
                    exponentials(j, range(2, 3))
                if m is not None:
                    wait(act, "tr2", m + 1)
                    wait(act, "gate_mm", m)
                    act.activation(hn2_t[:, :], dn[3][:, :], ACT.Identity, bias=col["ln2_b"],
                                   scale=col["ln2_g"]).then_inc(sem["hn2_t"], 1)
                if j is not None:
                    exponentials(j, range(3, NI))
                if a is not None:
                    mix_out(a, 1)
                if n is not None:
                    wait(act, "nmr1", n + 1)
                    wait(act, "hn_tr", n)
                    for g in range(NG):
                        act.activation(hn[:, g * P:(g + 1) * P], z[:, g * P:(g + 1) * P], ACT.Identity,
                                       bias=nmr[:, g:g + 1], scale=rs[:, 1, g:g + 1]).then_inc(sem["hn"], 1)
                if a is not None:
                    mix_out(a, 2)
                    mix_out(a, 3)
                if n is not None:
                    wait(act, "hn_tr", n + 1)
                    wait(act, "qkv_mm", 3 * n)
                    act.activation(hn_t[:, :], dn[2][:, :], ACT.Identity, bias=col["ln1_b"],
                                   scale=col["ln1_g"]).then_inc(sem["hn_t"], 1)
                    wait(act, "x1_tr", n + 1)
                    wait(act, "resid", n - 1)
                    act.activation(x1_tok[:, q, :], dn[3][:, :], ACT.Copy).then_inc(sem["x1_tok"], 1)
                    wait(act, "qkv_mm", 3 * n + 1)
                    wait(act, "s_mm", NI * n)
                    for h in range(HQ):
                        act.activation(kx[:, :, h, :], dn[1][:, :].rearrange("p (b s) -> p b s", s=S), ACT.Identity,
                                       bias=bk_mask[:, h:h + 1], scale=col["mask_h"][:, h:h + 1]).then_inc(sem["kx_out"], 1)
                if j is not None:
                    wait(act, "recip", j + 1)
                    wait(act, "rt_mm", j)
                    act.activation(rc[:, :, :], r64[:, :].unsqueeze(2).to_broadcast([P, NG * NH, D]),
                                   ACT.Copy).then_inc(sem["rcx"], 1)
                if n is not None:
                    wait(act, "qkv_mm", 3 * n + 2)
                    act.activation(qt[:, :], dn[0][:, :], ACT.Identity, bias=col["bq"]).then_inc(sem["q_out"], 1)
                if a is not None:
                    wait(act, "y_mm", a + 1)
                    wait(act, "yb2", a)
                    act.activation(yb[:, :], dn[2][:, :], ACT.Copy, scale=s_out[:, 0:1]).then_inc(sem["y_out"], 1)
                if j is not None:
                    wait(act, "pv_mm", j + 1)
                    wait(act, "o_t", j)
                    act.activation(acc[:, :, :], heads_out(0), ACT.Copy,
                                   scale=col["mask_h"][:, 0:1]).then_inc(sem["diag0"], 1)
                if n is not None:
                    wait(act, "qkv_mm", 3 * n + 3)
                    wait(act, "pv_mm", n)
                    act.activation(v[:, :, :], groups(dn[3][:, :]), ACT.Copy).then_inc(sem["v_out"], 1)

            def between(act):
                act.wait_ge(sem["setup2"], 5)

            act.wait_ge(sem["in8"], 32)
            act.activation(bias8f[:, :], bias8_in[:, :], ACT.Copy).then_inc(sem["bias8_out"], 1)
            act.wait_ge(sem["setup"], 6)
            run(act, iteration, between)
            moe_act(act)

        @block.vector
        def _(dve):
            setup_dve(dve)

            def norm(stats, mean_var, src, signal, count):
                for g in range(NG):
                    dve.bn_stats(stats[:, g, :], src(g)).then_inc(sem[signal], 1)
                wait(dve, signal, 2 * NG * count + NG)
                hold(dve, "held_dve")
                for g in range(NG):
                    dve.bn_aggr(mean_var[:, g, :], stats[:, g, :]).then_inc(sem[signal], 1)

            def pick(m):
                wait(dve, "gate_mm", m + 1)
                dve.tensor_tensor(lg[:, :, :], dn[0][:, 0:NG * E].rearrange("p (g e) -> p g e", e=E),
                                  over_groups(col["gate_b"]), ALU.add).then_inc(sem["pick"], 1)
                wait(dve, "pick", 6 * m + 1)
                dve.tensor_reduce(lmax[:, :], lg[:, :, :], AX.X, ALU.max).then_inc(sem["pick"], 1)
                wait(dve, "pick", 6 * m + 2)
                dve.tensor_tensor(oh[:, :, :], lg[:, :, :], lmax[:, :].unsqueeze(2).to_broadcast([P, NG, E]),
                                  ALU.is_equal).then_inc(sem["pick"], 1)
                wait(dve, "pick", 6 * m + 3)
                dve.tensor_tensor(lg[:, :, :], oh[:, :, :], over_groups(col["rank8"]),
                                  ALU.mult).then_inc(sem["pick"], 1)
                wait(dve, "pick", 6 * m + 4)
                dve.tensor_reduce(lmax[:, :], lg[:, :, :], AX.X, ALU.max).then_inc(sem["pick"], 1)
                wait(dve, "pick", 6 * m + 5)
                dve.tensor_tensor(oh_b[:, :, :], lg[:, :, :], lmax[:, :].unsqueeze(2).to_broadcast([P, NG, E]),
                                  ALU.is_equal).then_inc(sem["pick"], 1)

            def place(m, p):
                q = 1 - p
                wait(dve, "rank_mm", m + 1)
                dve.tensor_tensor(pos[:, :, :], dn[0][:, 64:64 + NG * E].rearrange("p (g e) -> p g e", e=E),
                                  over_groups(base[:, q, :]), ALU.add).then_inc(sem["slot"], 1)
                dve.tensor_tensor(base[:, p, :], dn[0][:, 64 + NG * E:64 + (NG + 1) * E], base[:, q, :],
                                  ALU.add).then_inc(sem["slot"], 1)
                wait(dve, "slot", 5 * m + 2)
                dve.tensor_tensor(pos[:, :, :], pos[:, :, :], oh_b[:, :, :], ALU.mult).then_inc(sem["slot"], 1)
                wait(dve, "slot", 5 * m + 3)
                dve.tensor_reduce(slot_f[:, :], pos[:, :, :], AX.X, ALU.add).then_inc(sem["slot"], 1)
                wait(dve, "slot", 5 * m + 4)
                wait(dve, "scattered", 16 * NG * m)
                dve.tensor_copy(slot[:, :], slot_f[:, :]).then_inc(sem["slot"], 1)

            def shifted(j, blocks):
                for i in blocks:
                    s = so[:, i, :].rearrange("p (n s) -> p n s", s=S)
                    m16 = mx[:, i * NG * HQ:(i + 1) * NG * HQ]
                    wait(dve, "s_mm", NI * j + i + 1)
                    dve.tensor_reduce(m16, s, AX.X, ALU.max).then_inc(sem["smax"], 1)
                    wait(dve, "smax", NI * j + i + 1)
                    wait(dve, "st", NI * j)
                    wait(dve, "sums", 3 * j)
                    dve.tensor_tensor(pr[:, i, :].rearrange("p (n s) -> p n s", s=S), s,
                                      m16.unsqueeze(2).to_broadcast([P, NG * HQ, S]),
                                      ALU.subtract).then_inc(sem["ssub"], 1)

            def other_head(j, h):
                wait(dve, "diag", 3 * j + h - 1)
                dve.scalar_tensor_tensor(acc[:, :, :], heads_out(h), col["mask_h"][:, h:h + 1], acc[:, :, :],
                                         ALU.mult, ALU.add).then_inc(sem["diag"], 1)

            def turned(j, i):
                wait(dve, "sexp", NI * j + i + 1)
                wait(dve, "pv_mm", j)
                dve.transpose(pt[:, i, :], pr[:, i, :]).then_inc(sem["st"], 1)

            def iteration(a, n, j, m, p):
                q = 1 - p
                if a is not None:
                    wait(dve, "h_mm", a + 1)
                    wait(dve, "u_mm", a)
                    dve.tensor_tensor(hs[:, :].rearrange("p (b s) -> p b s", s=S),
                                      dn[0][:, :].rearrange("p (b s) -> p b s", s=S),
                                      col["lora_w"][:, bass.ds(a * CB, CB)].unsqueeze(2).to_broadcast([P, CB, S]),
                                      ALU.mult).then_inc(sem["hs"], 1)
                if isinstance(a, int) and a == 0:
                    setup_k8_dve(dve)
                    setup2_dve(dve)
                if m is not None:
                    other_head(m, 3)
                    wait(dve, "diag", 3 * (m + 1))
                    wait(dve, "rt_mm", m + 1)
                    wait(dve, "wo_mm", m)
                    dve.tensor_tensor(o_t[:, :, :, :].rearrange("p g b s -> p b g s"),
                                      acc[:, :, :].rearrange("p (b g) s -> p b g s", b=GB),
                                      dn[1][:, :].rearrange("p (g b s) -> p b g s", g=NG, b=GB),
                                      ALU.mult).then_inc(sem["o_t"], 1)
                    wait(dve, "wo_mm", m + 1)
                    wait(dve, "zb", m + 1)
                    wait(dve, "resid", m)
                    wait(dve, "hn2", NG * m)
                    dve.tensor_tensor(xp[:, :], dn[3][:, :], zb[:, q, :], ALU.add).then_inc(sem["xp"], 1)
                    wait(dve, "xp", m + 1)
                    norm(bn2, mv2, lambda g: xp[:, g * P:(g + 1) * P], "ln2", m)
                if j is not None:
                    shifted(j, range(0, 1))
                if m is not None:
                    wait(dve, "rstd2", 2 * (m + 1))
                    dve.scalar_tensor_tensor(nmr2[:, :], mv2[:, :, 0], -1.0, rs2[:, 1, :], ALU.mult,
                                             ALU.mult).then_inc(sem["nmr2"], 1)
                if j is not None:
                    shifted(j, range(1, 2))
                if n is not None:
                    wait(dve, "z_mm", n + 1)
                    wait(dve, "zb", n)
                    wait(dve, "hn", NG * n)
                    dve.tensor_tensor(groups(z[:, :]), groups(dn[0][:, :]), over_groups(col["mix_bias"]),
                                      ALU.add).then_inc(sem["z"], 1)
                    wait(dve, "z", n + 1)
                    norm(bn, mv, lambda g: z[:, g * P:(g + 1) * P], "ln1", n)
                if j is not None:
                    shifted(j, range(2, 3))
                if n is not None:
                    wait(dve, "rstd1", 2 * (n + 1))
                    dve.scalar_tensor_tensor(nmr[:, :], mv[:, :, 0], -1.0, rs[:, 1, :], ALU.mult,
                                             ALU.mult).then_inc(sem["nmr1"], 1)
                if j is not None:
                    shifted(j, range(3, NI))
                if j is not None:
                    turned(j, 0)
                    turned(j, 1)
                if j is not None:
                    turned(j, 2)
                    turned(j, 3)
                if m is not None:
                    pick(m)
                if a is not None:
                    wait(dve, "uv", a + 1)
                    dve.tensor_scalar(magic[:, :].bitcast(U32), uv[:, :].bitcast(U32), 0x7F800000, 0x00400000,
                                      ALU.bitwise_and, ALU.bitwise_or).then_inc(sem["pow2"], 1)
                    wait(dve, "pow2", a + 1)
                    wait(dve, "gv", a + 1)
                    dve.scalar_tensor_tensor(gv[:, :], magic[:, :], 1.5 * 2.0 ** -6, gv[:, :], ALU.max,
                                             ALU.add).then_inc(sem["q8"], 1)
                if j is not None:
                    wait(dve, "sums", 3 * (j + 1))
                    dve.tensor_reduce(t1[:, :].rearrange("p (g i h) -> p i g h", g=NG, i=NI),
                                      t4[:, :, :].rearrange("p (i g h) s -> p i g h s", i=NI, g=NG), AX.X,
                                      ALU.add).then_inc(sem["rsum"], 1)
                    wait(dve, "rsum", j + 1)
                    wait(dve, "rcx", j)
                    dve.reciprocal(r64[:, :], t1[:, :]).then_inc(sem["recip"], 1)
                if a is not None:
                    wait(dve, "q8", 2 * a + 1)
                    wait(dve, "y_mm", a)
                    dve.scalar_tensor_tensor(q8[:, :], magic[:, :], 1.5 * 2.0 ** -6, gv[:, :], ALU.max,
                                             ALU.subtract).then_inc(sem["q8"], 1)
                if m is not None:
                    place(m, p)
                if a is not None:
                    if isinstance(a, int) and a == 0:
                        dve.wait_ge(sem["bias8_out"], 1)
                    wait(dve, "y_out", a + 1)
                    wait(dve, "x1", a)
                    dve.tensor_scalar(yb2[:, :], yb[:, :], bias8f[:, 0:1], None, ALU.add).then_inc(sem["yb2"], 1)
                if j is not None:
                    wait(dve, "diag0", j + 1)
                    other_head(j, 1)
                    other_head(j, 2)


            run(dve, iteration)
            moe_dve(dve)

        @block.gpsimd
        def _(pool):
            pool.memset(minus_half[:, :], -0.5).then_inc(sem["consts"], 1)
            pool.memset(pad[:, 0:2 * H], 0.0).then_inc(sem["consts"], 1)
            pool.memset(pad[:, 2 * H:ROW], PAD_ID).then_inc(sem["consts"], 1)
            pool.memset(ybd[:, :, :], 0.0).then_inc(sem["consts"], 1)
            for n in range(4):
                pool.memset(sched[f"c{n}"][:, :], 0.0).then_inc(sem["consts"], 1)
            pool.memset(sched["fours"][:, :], 0.0).then_inc(sem["consts"], 1)
            pool.wait_ge(sem["consts"], 9)

            def rstd(dst, mean_var, signal, source, count):
                wait(pool, source, 2 * NG * (count + 1))
                hold(pool, "held_pool")
                pool.tensor_scalar(dst[:, 0, :], mean_var[:, :, 1], EPS, 1.0, ALU.add, ALU.mult).then_inc(sem[signal], 1)
                wait(pool, signal, 2 * count + 1)
                pool.tensor_tensor(dst[:, 1, :], dst[:, 0, :], minus_half[:, :], ALU.pow).then_inc(sem[signal], 1)

            def iteration(a, n, j, m, p):
                q = 1 - p
                if isinstance(a, int) and a == 0:
                    pool.wait_ge(sem["in1"], 16)
                    pool.tensor_tensor(col["mix_w"], col["mix_w"], col["mix_mask"], ALU.mult).then_inc(sem["mix_masked"], 1)
                if a is not None:
                    wait(pool, "wb_mm", 4 * a)
                    hold(pool, "held_pool")
                    pool.tensor_tensor(ybd[:, :, :],
                                       col["y_rep"][:, bass.ds(a * CB, CB)].unsqueeze(1).to_broadcast([P, 16, CB]),
                                       col["mask_o"].unsqueeze(2).to_broadcast([P, 16, CB]),
                                       ALU.mult).then_inc(sem["ybd"], 1)
                if m is not None:
                    rstd(rs2, mv2, "rstd2", "ln2", m)
                    wait(pool, "xp", m + 1)
                    wait(pool, "x1_tok", m + 1)
                    wait(pool, "scattered", 16 * NG * m)
                    hold(pool, "held_pool")
                    pool.tensor_tensor(rows[:, :, H:2 * H], groups(x1_tok[:, q, :]), groups(xp[:, :]),
                                       ALU.add).then_inc(sem["resid"], 1)
                    pool.tensor_copy(rows[:, :, 2 * H], col["ids"][:, bass.ds(m * NG, NG)]).then_inc(sem["ids"], 1)
                if a is not None:
                    wait(pool, "uv", a + 1)
                    hold(pool, "held_pool")
                    pool.tensor_scalar(guard[:, :], uv[:, :], F32_MAX / FP8_MAX_IN, 0.0, ALU.mult,
                                       ALU.mult).then_inc(sem["guard"], 1)
                    wait(pool, "guard", a + 1)
                    wait(pool, "uvs", a + 1)
                    wait(pool, "q8", 2 * a)
                    pool.tensor_tensor(gv[:, :], uvs[:, :], guard[:, :], ALU.add).then_inc(sem["gv"], 1)
                if n is not None:
                    rstd(rs, mv, "rstd1", "ln1", n)
                if j is not None:
                    e32 = pr[:, :, :].rearrange("p i (n s) -> p (i n) s", s=S)
                    wait(pool, "sexp", NI * (j + 1))
                    pool.tensor_tensor(t16[:, :, :], e32[:, :, 0:16], e32[:, :, 16:32], ALU.add).then_inc(sem["sums"], 1)
                if j is not None:
                    wait(pool, "sums", 3 * j + 1)
                    pool.tensor_tensor(t8[:, :, :], t16[:, :, 0:8], t16[:, :, 8:16], ALU.add).then_inc(sem["sums"], 1)
                    wait(pool, "sums", 3 * j + 2)
                    wait(pool, "rsum", j)
                    pool.tensor_tensor(t4[:, :, :], t8[:, :, 0:4], t8[:, :, 4:8], ALU.add).then_inc(sem["sums"], 1)
                if n is not None:
                    wait(pool, "z", n + 1)
                    wait(pool, "xp", n - 1)
                    pool.wait_ge(sem["setup2"], 5)
                    pool.tensor_tensor(groups(zb[:, q, :]), groups(z[:, :]), over_groups(bo2[:, :]),
                                       ALU.add).then_inc(sem["zb"], 1)
                if m is not None:
                    wait(pool, "ids", m + 1)
                    wait(pool, "resid", m + 1)
                    wait(pool, "slot", 5 * (m + 1))
                    wait(pool, "hn2", NG * (m + 1))
                    hold(pool, "held_pool")
                    for g in range(NG):
                        pool.indirect_dma_start(routed, bass.IndirectOffsetOnAxis(slot[:, g:g + 1], 0),
                                                rows[:, g, :], None).then_inc(sem["scattered"], 16)
                if a is not None:
                    wait(pool, "yb2", a + 1)
                    wait(pool, "x1_tr", a - 1)
                    pool.tensor_tensor(x1[:, p, :], xb[:, p, :], yb2[:, :], ALU.add).then_inc(sem["x1"], 1)

            run(pool, iteration)
            moe_pool(pool)


def shape_constants():
    p = np.arange(P)
    c = {
        "ident": np.eye(P),
        "mask_o": (p[:, None] // G == np.arange(16)),
        "mask_h": (p[:, None] % 32 // D == np.arange(HQ)),
        "upper": (p[:, None] < p[None, :]),
        "ids": p[:, None] + P * np.arange(N_TOK // P),
        "region": np.broadcast_to(REGION * np.arange(E), (P, E)),
        "rank8": np.broadcast_to(E - np.arange(E), (P, E)),
        "tile_no": p[:, None],
        "tile_at": P * p[:, None],
        "octal": np.broadcast_to(8 ** (np.arange(4 * NF) % 4), (P, 4 * NF)),
        "expert_no": np.broadcast_to(np.arange(E), (P, E)),
    }
    return {k: np.ascontiguousarray(x, np.float32) for k, x in c.items()}


def kernel(**inputs):
    import concourse.bacc as bacc
    from concourse.bass_utils import run_bass_kernel_spmd

    a = {k: np.asarray(x) for k, x in inputs.items()}

    def rows(x):
        return np.broadcast_to(x.reshape(1, -1), (P, x.size))

    def column(x):
        return x.reshape(P, 1)

    w1 = a["L1_ffn_w1"].transpose(1, 0, 2)
    b1 = a["L1_ffn_b1"].reshape(E, FB, P).transpose(2, 0, 1)
    b2 = np.broadcast_to(a["L1_ffn_b2"], (P, E, H))
    parts = shape_constants() | {
        "lora_a": a["L0_cond_As"].reshape(P, H).T,
        "w_base": a["L0_cond_W_base"].T,
        "lora_b": a["L0_cond_Bs"].transpose(0, 2, 1).reshape(P, H),
        "lora_w": np.repeat(a["cond_8"].T, R, axis=0),
        "b_base": column(a["L0_cond_b_base"]),
        "s_in": rows(a["L0_ffn_input_scale"]),
        "s_k": rows(a["L0_ffn_kernel_scale"]),
        "y_rep": np.tile(a["cond_8"].T, (16, 1)),
        "mix_w": a["L1_cond_weight"].reshape(G, 8, 16, H).transpose(2, 0, 1, 3).reshape(P, G * H),
        "mix_mask": np.repeat(a["L1_cond_mask"].reshape(8, 16, H).transpose(1, 0, 2), G, axis=0).reshape(P, G * H),
        "wq": a["L1_ffn_wq"], "wk": a["L1_ffn_wk"], "wv": a["L1_ffn_wv"], "wo": a["L1_ffn_wo"],
        "gate_w": a["L1_ffn_gate_w"],
        "ln1_g": column(a["L1_ffn_ln1_g"]), "ln1_b": column(a["L1_ffn_ln1_b"]),
        "ln2_g": column(a["L1_ffn_ln2_g"]), "ln2_b": column(a["L1_ffn_ln2_b"]),
        "bq": column(a["L1_ffn_bq"]), "bk": column(a["L1_ffn_bk"]),
        "mix_bias": rows(a["L1_cond_bias"]), "bv": column(a["L1_ffn_bv"]), "bo": rows(a["L1_ffn_bo"]),
        "gate_b": rows(a["L1_ffn_gate_b"]),
        "w1": np.concatenate([w1, b1, b2], axis=2).reshape(P, E * W1_WIDTH),
        "w2": a["L1_ffn_w2"].reshape(E, FB, P, H).transpose(2, 0, 1, 3).reshape(P, E * F),
    }
    arrays = {f"pack{n}": np.ascontiguousarray(np.concatenate([parts[name] for name, _ in part], axis=1))
              for n, part in enumerate(PACK)}
    arrays["x_t"] = np.ascontiguousarray(a["x"].reshape(N_TOK, H).T)
    arrays["kernel8"] = np.ascontiguousarray(a["L0_ffn_kernel"])
    arrays["bias8"] = np.ascontiguousarray(a["L0_ffn_bias"].reshape(P, 1))

    nc = bacc.Bacc("TRN2", target_bir_lowering=False, num_devices=1)
    dram = {name: nc.dram_tensor(name, x.shape, mybir.dt.from_np(x.dtype), kind="ExternalInput").ap()
            for name, x in arrays.items()}
    out = nc.dram_tensor("out", (N_TOK, H), F32, kind="ExternalOutput").ap()
    build(nc, dram["x_t"], [dram[f"pack{n}"] for n in range(len(PACK))], dram["kernel8"], dram["bias8"], out)
    r = run_bass_kernel_spmd(nc, [arrays], core_ids=[0])
    return np.asarray(r.results[0]["out"]).reshape(B, S, H)
```
